# Optimizing a Trainium2 kernel written in Bass

```python
import numpy as np
import jax
import jax.numpy as jnp

def _softmax(x, axis=-1):
    return jax.nn.softmax(x, axis=axis)

def _gelu(x):
    return jax.nn.gelu(x, approximate=True)

def _silu(x):
    return jax.nn.silu(x)

def _sigmoid(x):
    return jax.nn.sigmoid(x)

def _layernorm(x, axis=-1, eps=1e-05):
    m = jnp.mean(x, axis=axis, keepdims=True)
    v = jnp.var(x, axis=axis, keepdims=True)
    return (x - m) / jnp.sqrt(v + eps)

def _scatter_add(tgt, idx, src, axis=0):
    return tgt.at[idx].add(src)

def _segment_sum(src, seg, n):
    return jax.ops.segment_sum(src, seg, n)
kernel_name = 'mk_adaln_d1_jaxref_r8_5775f3'

def setup_inputs(seed: int=0):
    np.random.seed(seed)
    _w = jnp.asarray

    def _L0_attn_setup():
        import jax, jax.numpy as jnp
        import numpy as np
        DT = 1.0
        N_HEAD = 16
        key = jax.random.key(seed)
        ks = jax.random.split(key, 10)
        B, T, D = (2, 256, 128)
        s = 1.0 / np.sqrt(D)
        return {'x': jax.random.normal(ks[0], (B, T, D), dtype=jnp.float32), 'Wq': jax.random.uniform(ks[1], (D, D), jnp.float32, -s, s), 'bq': jnp.zeros((D,), jnp.float32), 'Wk': jax.random.uniform(ks[2], (D, D), jnp.float32, -s, s), 'bk': jnp.zeros((D,), jnp.float32), 'Wv': jax.random.uniform(ks[3], (D, D), jnp.float32, -s, s), 'bv': jnp.zeros((D,), jnp.float32), 'Wo': jax.random.uniform(ks[4], (D, D), jnp.float32, -s, s), 'bo': jnp.zeros((D,), jnp.float32), 'alpha': jnp.float32(0.01)}
    _L0_attn_in = _L0_attn_setup()

    def _L0_ffn_setup():
        import jax, jax.numpy as jnp
        import numpy as np
        B, S, D = (2, 256, 128)
        E, K, F = (16, 2, 64)
        FS = 128
        key = jax.random.key(seed)
        ks = jax.random.split(key, 8)

        def w(k, shape, fan_in):
            return jax.random.normal(k, shape, jnp.float32) / np.sqrt(fan_in).astype(np.float32)
        return {'x': jax.random.normal(ks[0], (B, S, D), jnp.float32), 'Wr': w(ks[1], (D, E), D), 'Wg': w(ks[2], (E, D, F), D), 'Wu': w(ks[3], (E, D, F), D), 'Wd': w(ks[4], (E, F, D), F), 'Sg': w(ks[5], (D, FS), D), 'Su': w(ks[6], (D, FS), D), 'Sd': w(ks[7], (FS, D), FS)}
    _L0_ffn_in = _L0_ffn_setup()
    _L0_c = _w((lambda *s: np.random.randn(*s).astype(np.float32) * 0.05)(8, 128))
    _L0_wmod = _w((lambda *s: np.random.randn(*s).astype(np.float32) * 0.05)(128, 6 * 128) * 128 ** (-0.5))
    _d = {'L0_attn_x': _L0_attn_in['x'], 'L0_attn_Wq': _L0_attn_in['Wq'], 'L0_attn_bq': _L0_attn_in['bq'], 'L0_attn_Wk': _L0_attn_in['Wk'], 'L0_attn_bk': _L0_attn_in['bk'], 'L0_attn_Wv': _L0_attn_in['Wv'], 'L0_attn_bv': _L0_attn_in['bv'], 'L0_attn_Wo': _L0_attn_in['Wo'], 'L0_attn_bo': _L0_attn_in['bo'], 'L0_attn_alpha': _L0_attn_in['alpha'], 'L0_ffn_Wr': _L0_ffn_in['Wr'], 'L0_ffn_Wg': _L0_ffn_in['Wg'], 'L0_ffn_Wu': _L0_ffn_in['Wu'], 'L0_ffn_Wd': _L0_ffn_in['Wd'], 'L0_ffn_Sg': _L0_ffn_in['Sg'], 'L0_ffn_Su': _L0_ffn_in['Su'], 'L0_ffn_Sd': _L0_ffn_in['Sd'], 'L0_c': _L0_c, 'L0_wmod': _L0_wmod}
    _x0 = _d['L0_attn_x']
    _d['L0_attn_x'] = jax.random.normal(jax.random.fold_in(jax.random.key(seed), 1), (8, 256, 128), dtype=_x0.dtype)
    del _x0
    return _d

def reference(L0_attn_x, L0_attn_Wq, L0_attn_bq, L0_attn_Wk, L0_attn_bk, L0_attn_Wv, L0_attn_bv, L0_attn_Wo, L0_attn_bo, L0_attn_alpha, L0_ffn_Wr, L0_ffn_Wg, L0_ffn_Wu, L0_ffn_Wd, L0_ffn_Sg, L0_ffn_Su, L0_ffn_Sd, L0_c, L0_wmod):

    def _L0_attn_ref(x, Wq, bq, Wk, bk, Wv, bv, Wo, bo, alpha):
        import jax, jax.numpy as jnp
        import numpy as np
        DT = 1.0
        N_HEAD = 16
        B, T, D = x.shape
        H = N_HEAD
        hd = D // H
        scale = hd ** (-0.5)
        q = (x @ Wq.T + bq).reshape(B, T, H, hd)
        k = (x @ Wk.T + bk).reshape(B, T, H, hd)
        v = (x @ Wv.T + bv).reshape(B, T, H, hd)
        scores = jnp.einsum('bqhd,bkhd->bhqk', q, k) * scale
        idx = jnp.arange(T)
        lag = jnp.abs(idx[:, None] - idx[None, :]).astype(jnp.float32)
        decay = jnp.exp(-alpha * lag * DT)
        scores = scores * decay
        attn = jax.nn.softmax(scores, axis=-1)
        out = jnp.einsum('bhqk,bkhd->bqhd', attn, v).reshape(B, T, D)
        return out @ Wo.T + bo

    def _L0_ffn_ref(x, Wr, Wg, Wu, Wd, Sg, Su, Sd):
        import jax, jax.numpy as jnp
        import numpy as np
        B, S, D = (2, 256, 128)
        E, K, F = (16, 2, 64)
        FS = 128
        b, s, d = x.shape
        T = b * s
        xf = x.reshape(T, d)
        shared = jax.nn.silu(xf @ Sg) * (xf @ Su) @ Sd
        probs = jax.nn.softmax(xf @ Wr, axis=-1)
        topk_p, topk_i = jax.lax.top_k(probs, K)
        n_exp = Wr.shape[1]
        cw = jnp.zeros((T, n_exp), x.dtype).at[jnp.arange(T)[:, None], topk_i].add(topk_p)

        def step(acc, ew):
            wg, wu, wd, c = ew
            y = jax.nn.silu(xf @ wg) * (xf @ wu) @ wd
            return (acc + y * c[:, None], None)
        routed, _ = jax.lax.scan(step, jnp.zeros_like(xf), (Wg, Wu, Wd, cw.T))
        return (routed + shared).reshape(b, s, d)
    x = L0_attn_x
    mod = (_silu(L0_c) @ L0_wmod).reshape(L0_c.shape[0], 6, 1, -1)
    sa, ca, ga, sb, cb, gb = (mod[:, 0], mod[:, 1], mod[:, 2], mod[:, 3], mod[:, 4], mod[:, 5])
    ga = (2 * (ga >= 0) - 1) * jnp.maximum(jnp.abs(ga), 0.25)
    gb = (2 * (gb >= 0) - 1) * jnp.maximum(jnp.abs(gb), 0.25)
    h = _layernorm(x, axis=-1) * (1 + ca) + sa
    x = x + ga * _L0_attn_ref(h, L0_attn_Wq, L0_attn_bq, L0_attn_Wk, L0_attn_bk, L0_attn_Wv, L0_attn_bv, L0_attn_Wo, L0_attn_bo, L0_attn_alpha)
    h = _layernorm(x, axis=-1) * (1 + cb) + sb
    x = x + gb * _L0_ffn_ref(h, L0_ffn_Wr, L0_ffn_Wg, L0_ffn_Wu, L0_ffn_Wd, L0_ffn_Sg, L0_ffn_Su, L0_ffn_Sd)
    return x

_drawn_inputs = setup_inputs


def setup_inputs(seed=0):
    import zlib

    import numpy as np

    out = dict(_drawn_inputs(seed))
    spreads = {'L0_attn_bq': (0.0, 0.8),
     'L0_attn_bk': (0.0, 0.8),
     'L0_attn_bv': (0.0, 0.564),
     'L0_attn_bo': (0.0, 0.313)}
    factors = {'L0_attn_Wq': 8.0,
     'L0_attn_Wk': 8.0,
     'L0_attn_Wv': 8.0,
     'L0_attn_Wo': 3.802,
     'L0_ffn_Wr': 3.323,
     'L0_ffn_Wg': 3.324,
     'L0_ffn_Wu': 3.144,
     'L0_ffn_Wd': 3.139}
    for name, (base, spread) in spreads.items():
        noise = np.random.default_rng([zlib.crc32(name.encode()), seed]).standard_normal(out[name].shape)
        drawn = base * np.exp(spread * noise) if base else spread * noise
        out[name] = jnp.asarray(drawn.astype(out[name].dtype))
    for name, factor in factors.items():
        out[name] = (out[name] * factor).astype(out[name].dtype)
    return out
```

```python
from contextlib import ExitStack

import numpy as np

import concourse.bass as bass
from concourse import mybir

F32 = mybir.dt.float32
F32R = mybir.dt.float32r
BF16 = mybir.dt.bfloat16
ALU = mybir.AluOpType
ACT = mybir.ActivationFunctionType
AX_X = mybir.AxisListType.X

P = 128
NB, SEQ, D = 8, 256, 128
HEADS, HD = 16, 8
E, FE, FS = 16, 64, 128
EPS = 1e-5
CHUNK = 512
NCHUNK = NB * SEQ // CHUNK
TT = CHUNK // P
BPC = CHUNK // SEQ
QUAD = 4
NG = HEADS // QUAD
STEPS = BPC * HEADS
QUADS = STEPS // QUAD
SLOTS = 4
VW = 32
NU = E * FE // P + FS // P
STACK = 2 * SLOTS * 16
RING = 8
FR = 3
NEG = -3.0e38

LAG_T, LAG_PV = 3, 8


def build(nc, x, c_t, wq_t, wk_t, wv_t, wo_t, b_q, b_k, b_v, b_o, alpha, w_r, w_gu, w_d, w_mod,
          lag, ident, sel_b, sel_e, out):
    x_v = x.rearrange("(n p) d -> p n d", p=P)
    out_v = out.rearrange("(n p) d -> p n d", p=P)

    with ExitStack() as ctx:
        def sb(name, shape, dt=F32):
            return ctx.enter_context(nc.sbuf_tensor(name, shape, dt))

        def sem(name):
            return ctx.enter_context(nc.semaphore(name))

        id_f = sb("id_f", [P, P])
        id_b = sb("id_b", [P, P], BF16)
        decay = sb("decay", [P, BPC, SEQ])
        alpha_sb = sb("alpha_sb", [P, 1])
        nalpha = sb("nalpha", [P, 1])
        wq_sb, wk_sb, wv_sb, wo_sb = (sb(n, [P, D]) for n in ("wq_sb", "wk_sb", "wv_sb", "wo_sb"))
        bq_sb, bk_sb = sb("bq_sb", [P, 1]), sb("bk_sb", [P, 1])
        bv_sb, bo_sb = sb("bv_sb", [P, D]), sb("bo_sb", [P, D])
        wr_sb = sb("wr_sb", [P, E])
        wgu_sb = sb("wgu_sb", [P, NU, 2, P])
        wgu_hi = sb("wgu_hi", [P, NU, 2, P], F32R)
        wgu_lo = sb("wgu_lo", [P, NU, 2, P], F32R)
        wd_sb = sb("wd_sb", [P, NU, D])
        wmod_sb = sb("wmod_sb", [P, 6, D])
        selb_sb = sb("selb_sb", [NB, NB, P])
        sele_f = sb("sele_f", [3 * E, NU - 1, P])
        sele_b = sb("sele_b", [3 * E, NU - 1, P], BF16)
        ct_sb, silu_c = sb("ct_sb", [P, NB]), sb("silu_c", [P, NB])
        mod_t = sb("mod_t", [P, 4, NB])
        gate8, gate8s, gate8m = (sb(n, [NB, 2, D]) for n in ("gate8", "gate8s", "gate8m"))
        gates = sb("gates", [P, NB, 2, D])
        nhalf = sb("nhalf", [P, TT])
        x_all = sb("x_all", [P, NCHUNK * TT, D])
        stats, mv, var_e, rstd = (sb("stats", [P, TT, 6]), sb("mv", [P, TT, 2]),
                                  sb("var_e", [P, TT]), sb("rstd", [P, TT]))
        stats2, mv2, var_e2, rstd2 = (sb("stats2", [P, TT, 6]), sb("mv2", [P, TT, 2]),
                                      sb("var_e2", [P, TT]), sb("rstd2", [P, TT]))
        xn, xn2 = sb("xn", [P, TT, D]), sb("xn2", [P, TT, D])
        h_t, h2_t = sb("h_t", [P, CHUNK]), sb("h2_t", [P, CHUNK])
        h2_hi = sb("h2_hi", [P, NCHUNK, CHUNK], F32R)
        h2_lo = sb("h2_lo", [P, NCHUNK, CHUNK], F32R)
        qk_hi = sb("qk_hi", [P, 2, CHUNK], F32R)
        qk_lo = sb("qk_lo", [P, 2, CHUNK], F32R)
        q_st = sb("q_st", [P, NG, CHUNK], F32R)
        k_st = sb("k_st", [P, NG, CHUNK], F32R)
        v_nat = sb("v_nat", [P, TT, NG, QUAD, HD])
        v_one = sb("v_one", [P, TT, NG, QUAD, VW])
        sc = sb("sc", [P, RING, BPC, SEQ])
        mx = sb("mx", [P, RING, BPC])
        pr = sb("pr", [P, RING, BPC, SEQ])
        o_t = sb("o_t", [P, 2, CHUNK])
        rsum = sb("rsum", [P, TT, QUAD])
        attn = sb("attn", [P, TT, NG, QUAD, HD])
        attn_t = sb("attn_t", [P, CHUNK])
        res = sb("res", [P, TT, D])
        lg = sb("lg", [P, TT, E + 8])
        top8 = sb("top8", [P, TT, 8])
        struck = sb("struck", [P, TT, E + 8])
        ex, rz, zs = sb("ex", [P, TT, E]), sb("rz", [P, TT]), sb("zs", [P, TT])
        cw = sb("cw", [P, TT, E])
        cwp = sb("cwp", [P, TT, 3, E], BF16)
        cw_t = sb("cw_t", [3 * E, NCHUNK, CHUNK], BF16)
        act_g = sb("act_g", [P, FR, CHUNK])
        act_u = sb("act_u", [P, FR, CHUNK])
        act = sb("act", [P, FR, CHUNK])

        bank = [ctx.enter_context(nc.psum_tensor(f"bank{i}", [P, CHUNK], F32)) for i in range(8)]
        ps_s, ps_t, ps_o, ps_a, ps_b = bank[0:2], bank[2:4], bank[4:6], bank[6], bank[7]
        ps_g, ps_u, ps_c, ps_y = bank[0:3], bank[3:6], bank[6], bank[7]

        s = {n: sem(n) for n in (
            "ld_x0 ld_x ld_w ld_w2 ld_late alpha_ok decay_raw decay_ok silu_ok modt_mm modt_ok gate_mm gate8_a gate8_b "
            "gate8_c gate8_ok gateb_mm gates_ok idb_ok vone_ok pool_init lg_init whi_ok wlo_ok sele_ok "
            "stats_ok mv_ok vare_ok rstd_ok xn_ok lnt_done h_ok qk_mm qk_hi_ok qk_lo_ok v_mm v_ok vgrp_ok "
            "s_done ttr_done nd_done t_done exp_done pv_done ot_ok c_done rs_ok norm_ok "
            "at_done at_ok wo_done res_a res_b x2_ok stats2_ok mv2_ok vare2_ok rstd2_ok xn2_ok ln2t_done "
            "h2t_ok h2hi_ok h2lo_ok r_done lg_ok top_ok fill_ok ls_ok struck_ok ex_ok zs_ok rz_ok em_ok "
            "cw_ok cp0_ok cp1_ok r1_ok cp_ok cwt_done cwt_ok "
            "gate_done up_done cb_done silu_done mul_done act_ok down_done y_scaled y_free").split()}
        s_st = [sem(f"stacked{g}") for g in range(NG)]
        s_out = sem("out_written")
        begun = {e: sem(f"begun{k}") for k, e in enumerate((nc.vector, nc.gpsimd, nc.tensor))}

        block = ctx.enter_context(nc.Block())

        def begin(eng, i):
            if not isinstance(i, int):
                eng.sem_inc(begun[eng])

        def mod2(ap):
            return ap.rearrange("p (b t) d -> p b t d", b=BPC)

        @block.sync
        def _(sp):
            for ap, dram in ((ct_sb[:], c_t), (wmod_sb[:], w_mod), (selb_sb[:], sel_b)):
                sp.dma_start(ap, dram).then_inc(s["ld_w"], 16)
            sp.dma_start(x_all[:, 0:TT, :], x_v[:, 0:TT, :]).then_inc(s["ld_x0"], 16)
            for ap, dram in ((id_f[:], ident), (wq_sb[:], wq_t), (wk_sb[:], wk_t), (wv_sb[:], wv_t),
                             (bq_sb[:], b_q), (bk_sb[:], b_k), (bv_sb[:], b_v.to_broadcast([P, D])),
                             (decay[:], lag), (alpha_sb[:], alpha.to_broadcast([P, 1]))):
                sp.dma_start(ap, dram).then_inc(s["ld_w2"], 16)
            sp.dma_start(x_all[:, TT:, :], x_v[:, TT:, :]).then_inc(s["ld_x"], 16)
            for ap, dram in ((wo_sb[:], wo_t), (bo_sb[:], b_o.to_broadcast([P, D])), (wr_sb[:], w_r),
                             (sele_f[:], sel_e), (wgu_sb[:], w_gu), (wd_sb[:], w_d)):
                sp.dma_start(ap, dram).then_inc(s["ld_late"], 16)

            def stack(c, g, reused):
                if g == 0 or not reused:
                    sp.wait_ge(s["qk_lo_ok"], c * 2 + 2)
                if reused:
                    sp.wait_ge(s["s_done"], (c - 1) * STEPS + 8 * g + 8)
                for i, dst in enumerate((q_st, k_st)):
                    for slot in range(SLOTS):
                        half = slot // 2 if i == 0 else slot % 2
                        src = (qk_hi, qk_lo)[half][32 * g:32 * g + 32, i, :].bitcast(F32)
                        sp.dma_start(dst[slot:P:SLOTS, g, :].bitcast(F32), src).then_inc(s_st[g], 16)

            def chunk(i, nxt, first=False):
                stack(i, 3, reused=not first)
                if nxt:
                    for g in range(3):
                        stack(i + 1, g, reused=True)

            for g in range(3):
                stack(0, g, reused=False)
            chunk(0, True, first=True)
            with sp.Fori(1, NCHUNK - 1) as i:
                chunk(i, True)
            chunk(NCHUNK - 1, False)

            with sp.Fori(0, NCHUNK) as i:
                sp.wait_ge(s["y_free"], i + 2)
                sp.dma_start(out_v[:, bass.ds(i * TT, TT), :],
                             x_all[:, bass.ds(i * TT, TT), :]).then_inc(s_out, 16)
            sp.wait_ge(s_out, 16 * NCHUNK)

        @block.gpsimd
        def _(pool):
            nc.gpsimd.memset(nhalf[:], -0.5).then_inc(s["pool_init"], 1)
            nc.gpsimd.memset(v_one[:], 0.0).then_inc(s["pool_init"], 1)
            pool.wait_ge(s["pool_init"], 2)
            nc.gpsimd.memset(v_one[:, :, :, :, HD:HD + 1], 1.0).then_inc(s["vone_ok"], 1)
            nc.gpsimd.memset(lg[:], NEG).then_inc(s["lg_init"], 1)

            def rstd_of(c, mv_, var_, rstd_, ready, mid, done):
                pool.wait_ge(s[ready], c + 1)
                begin(pool, c)
                nc.gpsimd.tensor_scalar(var_[:], mv_[:, :, 1], 1.0, EPS, ALU.mult, ALU.add).then_inc(s[mid], 1)
                pool.wait_ge(s[mid], c + 1)
                nc.gpsimd.tensor_tensor(rstd_[:], var_[:], nhalf[:], ALU.pow).then_inc(s[done], 1)

            def ln1(c):
                rstd_of(c, mv, var_e, rstd, "mv_ok", "vare_ok", "rstd_ok")

            def ln2(c):
                rstd_of(c, mv2, var_e2, rstd2, "mv2_ok", "vare2_ok", "rstd2_ok")

            def chunk(i, cur, prev, nxt):
                for n in range(STEPS if cur else 12):
                    if cur:
                        pool.wait_ge(s["ttr_done"], i * STEPS + n + 1)
                        begin(pool, i)
                        for t in range(BPC):
                            last = nc.gpsimd.tensor_scalar(sc[:, n % RING, t, :], sc[:, n % RING, t, :], -1.0,
                                                           mx[:, n % RING, t:t + 1], ALU.mult, ALU.add)
                        last.then_inc(s["nd_done"], 1)
                    if n == 4 and nxt:
                        ln1(i + 1)
                    if n == 11 and prev:
                        ln2(i - 1)

            ln1(0)
            chunk(0, True, False, True)
            with pool.Fori(1, NCHUNK - 1) as i:
                chunk(i, True, True, True)
            chunk(NCHUNK - 1, True, True, False)
            chunk(NCHUNK, False, True, False)

        @block.scalar
        def _(act_e):
            def modulated(dst, src, c, shift, b):
                at = c * BPC + b
                nc_at = bass.ds(at, 1)
                return nc.scalar.activation(dst, src, ACT.Identity, bias=mod_t[:, shift, nc_at],
                                            scale=mod_t[:, shift + 1, nc_at])

            def h1(c):
                act_e.wait_ge(s["lnt_done"], c + 1)
                for b in range(BPC):
                    r = slice(b * SEQ, b * SEQ + SEQ)
                    last = modulated(h_t[:, r], ps_b[:, r], c, 0, b)
                last.then_inc(s["h_ok"], 1)

            def qk_hi_of(c, i, reused):
                act_e.wait_ge(s["qk_mm"], c * 2 + i + 1)
                if reused and i == 0:
                    act_e.wait_ge(s_st[NG - 1], c * STACK)
                nc.scalar.activation(qk_hi[:, i, :], ps_b[:], ACT.Identity, bias=(bq_sb, bk_sb)[i][:, 0:1],
                                     scale=1.0).then_inc(s["qk_hi_ok"], 1)

            def v_group(c, g, reused):
                act_e.wait_ge(s["v_ok"], c + 1)
                if reused:
                    act_e.wait_ge(s["pv_done"], (c - 1) * QUADS + 2 * g + 2)
                nc.scalar.activation(v_one[:, :, g, :, 0:HD], v_nat[:, :, g, :, :],
                                     ACT.Copy).then_inc(s["vgrp_ok"], 1)

            def out_t(c, g, first):
                act_e.wait_ge(s["pv_done"], c * QUADS + 2 * g + 2)
                if not (first and g < 2):
                    act_e.wait_ge(s["c_done"], c * NG + g - 1)
                nc.scalar.activation(o_t[:, g % 2, :], ps_o[g % 2][:], ACT.Copy).then_inc(s["ot_ok"], 1)

            def chunk(i, cur, prev, nxt):
                for n in range(STEPS if cur else 24):
                    m, own = n - LAG_T, n >= LAG_T
                    if (own and cur) or (prev and not own):
                        base = (i if own else i - 1) * STEPS + m % STEPS
                        m %= STEPS
                        act_e.wait_ge(s["t_done"], base + 1)
                        if m % QUAD == 0 and (prev or m >= RING):
                            act_e.wait_ge(s["pv_done"], (i if own else i - 1) * QUADS + m // QUAD - 1)
                        nc.scalar.activation(pr[:, m % RING, :, :].rearrange("p a b -> p (a b)"), ps_t[m % 2][:],
                                             ACT.Exp, scale=-1.0).then_inc(s["exp_done"], 1)
                    if n == 5 and prev:
                        out_t(i - 1, 3, False)
                    if n == 5 and cur:
                        v_group(i, 3, prev)
                    if n == 8 and prev:
                        act_e.wait_ge(s["at_done"], i)
                        nc.scalar.activation(attn_t[:], ps_b[:], ACT.Copy).then_inc(s["at_ok"], 1)
                    if n == 9 and nxt:
                        h1(i + 1)
                    if n == 11 and nxt:
                        qk_hi_of(i + 1, 0, True)
                    if n == 13 and nxt:
                        qk_hi_of(i + 1, 1, True)
                    if n in (13, 21, 29) and cur:
                        out_t(i, (n - 13) // 8, not prev)
                    if n == 14 and prev:
                        act_e.wait_ge(s["ln2t_done"], i)
                        for b in range(BPC):
                            r = slice(b * SEQ, b * SEQ + SEQ)
                            last = modulated(h2_t[:, r], ps_a[:, r], i - 1, 2, b)
                        last.then_inc(s["h2t_ok"], 1)
                        for b in range(BPC):
                            r = slice(b * SEQ, b * SEQ + SEQ)
                            dst = h2_hi[:, bass.ds(i - 1, 1), r].rearrange("p a n -> p (a n)")
                            last = modulated(dst, ps_a[:, r], i - 1, 2, b)
                        last.then_inc(s["h2hi_ok"], 1)
                    if n == 18 and prev:
                        act_e.wait_ge(s["ls_ok"], i)
                        nc.scalar.activation(ex[:], ex[:], ACT.Exp).then_inc(s["ex_ok"], 1)
                    if n == 20 and prev:
                        act_e.wait_ge(s["cwt_done"], i)
                        nc.scalar.activation(cw_t[:, bass.ds(i - 1, 1), :].rearrange("p a n -> p (a n)"),
                                             ps_b[0:3 * E, 0:CHUNK // 2].bitcast(BF16),
                                             ACT.Copy).then_inc(s["cwt_ok"], 1)
                    if n in (24, 25, 30) and nxt:
                        v_group(i + 1, {24: 0, 25: 1, 30: 2}[n], True)
                    if n == 26 and cur and not prev:
                        act_e.wait_ge(s["ld_late"], 16 * 6)
                        nc.scalar.activation(wgu_hi[:], wgu_sb[:], ACT.Copy).then_inc(s["whi_ok"], 1)

            act_e.wait_ge(s["ld_w"], 48)
            nc.scalar.activation(silu_c[:], ct_sb[:], ACT.Silu).then_inc(s["silu_ok"], 1)
            act_e.wait_ge(s["ld_w2"], 16 * 9)
            act_e.wait_ge(s["alpha_ok"], 1)
            nc.scalar.activation(decay[:], decay[:], ACT.Exp, scale=nalpha[:, 0:1]).then_inc(s["decay_raw"], 1)
            act_e.wait_ge(s["modt_ok"], 2)
            h1(0)
            qk_hi_of(0, 0, False)
            qk_hi_of(0, 1, False)
            act_e.wait_ge(s["vone_ok"], 1)
            for g in range(3):
                v_group(0, g, False)
            chunk(0, True, False, True)
            with act_e.Fori(1, NCHUNK - 1) as i:
                chunk(i, True, True, True)
            chunk(NCHUNK - 1, True, True, False)
            chunk(NCHUNK, False, True, False)

            with act_e.Fori(0, NCHUNK) as i:
                for u in range(NU):
                    act_e.wait_ge(s["gate_done"], i * NU + u + 1)
                    act_e.wait_ge(s["act_ok"], i * NU + u + 1)
                    nc.scalar.activation(act_g[:, u % FR, :], ps_g[u % FR][:], ACT.Silu).then_inc(s["silu_done"], 1)

        @block.vector
        def _(dve):
            def ln_stats(c, st, mv_, sem_st, sem_mv):
                begin(dve, c)
                for t in range(TT):
                    src = x_all[:, bass.ds(c * TT + t, 1), :].rearrange("p a d -> p (a d)")
                    last = nc.vector.bn_stats(st[:, t, :], src)
                last.then_inc(s[sem_st], 1)
                dve.wait_ge(s[sem_st], c + 1)
                begin(dve, c)
                for t in range(TT):
                    last = nc.vector.bn_aggr(mv_[:, t, :], st[:, t, :])
                last.then_inc(s[sem_mv], 1)

            def ln_apply(c, mv_, rstd_, dst, sem_r, sem_x):
                dve.wait_ge(s[sem_r], c + 1)
                for t in range(TT):
                    src = x_all[:, bass.ds(c * TT + t, 1), :].rearrange("p a d -> p (a d)")
                    last = nc.vector.tensor_scalar(dst[:, t, :], src, mv_[:, t, 0:1], rstd_[:, t:t + 1],
                                                   ALU.subtract, ALU.mult)
                last.then_inc(s[sem_x], 1)

            def qk_lo_of(c, i):
                dve.wait_ge(s["qk_hi_ok"], c * 2 + i + 1)
                nc.vector.scalar_tensor_tensor(qk_lo[:, i, :], ps_b[:], (bq_sb, bk_sb)[i][:, 0:1],
                                               qk_hi[:, i, :].bitcast(F32), ALU.add,
                                               ALU.subtract).then_inc(s["qk_lo_ok"], 1)

            def v_bias(c, reused):
                dve.wait_ge(s["v_mm"], c + 1)
                if reused:
                    dve.wait_ge(s["vgrp_ok"], c * NG)
                nc.vector.tensor_tensor(v_nat[:].rearrange("p t g j d -> p t (g j d)"),
                                        ps_b[:].rearrange("p (t d) -> p t d", t=TT),
                                        bv_sb[:].unsqueeze(1).to_broadcast([P, TT, D]), ALU.add).then_inc(s["v_ok"], 1)

            def norm(c, g, first):
                src = ps_a[:].rearrange("p (t j w) -> p t j w", t=TT, j=QUAD)
                dve.wait_ge(s["c_done"], c * NG + g + 1)
                nc.vector.reciprocal(rsum[:], src[:, :, :, HD]).then_inc(s["rs_ok"], 1)
                dve.wait_ge(s["rs_ok"], c * NG + g + 1)
                if g == 0 and not first:
                    dve.wait_ge(s["at_done"], c)
                nc.vector.tensor_tensor(attn[:, :, g, :, :], src[:, :, :, 0:HD],
                                        rsum[:].unsqueeze(3).to_broadcast([P, TT, QUAD, HD]),
                                        ALU.mult).then_inc(s["norm_ok"], 1)

            def residual(c):
                dve.wait_ge(s["wo_done"], c + 1)
                nc.vector.tensor_tensor(res[:], ps_a[:].rearrange("p (t d) -> p t d", t=TT),
                                        bo_sb[:].unsqueeze(1).to_broadcast([P, TT, D]), ALU.add).then_inc(s["res_a"], 1)
                dve.wait_ge(s["res_a"], c + 1)
                ga = gates[:, bass.ds(c * BPC, BPC), 0, :].unsqueeze(2).to_broadcast([P, BPC, TT // BPC, D])
                nc.vector.tensor_tensor(mod2(res[:]), mod2(res[:]), ga, ALU.mult).then_inc(s["res_b"], 1)
                dve.wait_ge(s["res_b"], c + 1)
                xs = x_all[:, bass.ds(c * TT, TT), :]
                nc.vector.tensor_tensor(xs, xs, res[:], ALU.add).then_inc(s["x2_ok"], 1)
                dve.wait_ge(s["x2_ok"], c + 1)

            def logits(c):
                dve.wait_ge(s["r_done"], c + 1)
                nc.vector.tensor_copy(lg[:, :, 0:E],
                                      ps_a[:, 0:TT * E].rearrange("p (t e) -> p t e", t=TT)).then_inc(s["lg_ok"], 1)
                dve.wait_ge(s["lg_ok"], c + 1)
                begin(dve, c)
                for t in range(TT):
                    last = nc.vector.max(top8[:, t, :], lg[:, t, 0:E])
                last.then_inc(s["top_ok"], 1)
                dve.wait_ge(s["top_ok"], c + 1)
                nc.vector.tensor_tensor(ex[:], lg[:, :, 0:E], top8[:, :, 0:1].to_broadcast([P, TT, E]),
                                        ALU.subtract).then_inc(s["ls_ok"], 1)
                dve.wait_ge(s["ls_ok"], c + 1)
                nc.vector.memset(top8[:, :, 2:8], NEG).then_inc(s["fill_ok"], 1)
                dve.wait_ge(s["fill_ok"], c + 1)
                begin(dve, c)
                for t in range(TT):
                    last = nc.vector.match_replace(struck[:, t, :], top8[:, t, :], lg[:, t, :], 3.0e38)
                last.then_inc(s["struck_ok"], 1)

            def weights(c):
                dve.wait_ge(s["ex_ok"], c + 1)
                nc.vector.tensor_reduce(zs[:], ex[:], AX_X, ALU.add).then_inc(s["zs_ok"], 1)
                dve.wait_ge(s["struck_ok"], c + 1)
                nc.vector.tensor_tensor(cw[:], struck[:, :, 0:E], lg[:, :, 0:E], ALU.not_equal).then_inc(s["em_ok"], 1)
                dve.wait_ge(s["zs_ok"], c + 1)
                nc.vector.reciprocal(rz[:], zs[:]).then_inc(s["rz_ok"], 1)
                dve.wait_ge(s["em_ok"], 2 * c + 1)
                nc.vector.tensor_tensor(cw[:], cw[:], ex[:], ALU.mult).then_inc(s["em_ok"], 1)
                dve.wait_ge(s["em_ok"], 2 * c + 2)
                dve.wait_ge(s["rz_ok"], c + 1)
                nc.vector.tensor_tensor(cw[:], cw[:], rz[:].unsqueeze(2).to_broadcast([P, TT, E]),
                                        ALU.mult).then_inc(s["cw_ok"], 1)
                dve.wait_ge(s["cw_ok"], c + 1)
                nc.vector.tensor_copy(cwp[:, :, 0, :], cw[:]).then_inc(s["cp0_ok"], 1)
                dve.wait_ge(s["cp0_ok"], c + 1)
                nc.vector.tensor_tensor(cw[:], cw[:], cwp[:, :, 0, :], ALU.subtract).then_inc(s["r1_ok"], 1)
                dve.wait_ge(s["r1_ok"], c + 1)
                nc.vector.tensor_copy(cwp[:, :, 1, :], cw[:]).then_inc(s["cp1_ok"], 1)
                dve.wait_ge(s["cp1_ok"], c + 1)
                nc.vector.tensor_tensor(cwp[:, :, 2, :], cw[:], cwp[:, :, 1, :], ALU.subtract).then_inc(s["cp_ok"], 1)

            def chunk(i, cur, prev, nxt):
                for n in range(STEPS if cur else 24):
                    if cur:
                        dve.wait_ge(s["s_done"], i * STEPS + n + 1)
                        if prev or n >= RING:
                            dve.wait_ge(s["t_done"], i * STEPS + n - RING + 1)
                        begin(dve, i)
                        for t in range(BPC):
                            last = nc.vector.tensor_tensor_reduce(
                                sc[:, n % RING, t, :], ps_s[n % 2][:, t * SEQ:t * SEQ + SEQ], decay[:, t, :],
                                1.0, NEG, ALU.mult, ALU.max, mx[:, n % RING, t:t + 1])
                        last.then_inc(s["ttr_done"], 1)
                    if n == 3 and nxt:
                        ln_stats(i + 1, stats, mv, "stats_ok", "mv_ok")
                    if n == 7 and nxt:
                        ln_apply(i + 1, mv, rstd, xn, "rstd_ok", "xn_ok")
                    if n == 7 and prev:
                        norm(i - 1, 3, False)
                    if n == 11 and prev:
                        residual(i - 1)
                        ln_stats(i - 1, stats2, mv2, "stats2_ok", "mv2_ok")
                    if n == 12 and nxt:
                        qk_lo_of(i + 1, 0)
                    if n == 13 and prev:
                        ln_apply(i - 1, mv2, rstd2, xn2, "rstd2_ok", "xn2_ok")
                    if n == 14 and nxt:
                        qk_lo_of(i + 1, 1)
                    if n == 15 and prev:
                        dve.wait_ge(s["h2hi_ok"], i)
                        dst, hi = (a[:, bass.ds(i - 1, 1), :].rearrange("p a n -> p (a n)") for a in (h2_lo, h2_hi))
                        nc.vector.tensor_tensor(dst, h2_t[:], hi.bitcast(F32), ALU.subtract).then_inc(s["h2lo_ok"], 1)
                    if n == 17 and prev:
                        logits(i - 1)
                    if n == 19 and prev:
                        weights(i - 1)
                    if n == 19 and cur:
                        norm(i, 0, not prev)
                    if n == 23 and nxt:
                        v_bias(i + 1, True)
                    if n == 25 and cur:
                        norm(i, 1, not prev)
                    if n == 31 and cur:
                        norm(i, 2, not prev)
                    if n == 28 and cur and not prev:
                        dve.wait_ge(s["whi_ok"], 1)
                        nc.vector.tensor_tensor(wgu_lo[:], wgu_sb[:], wgu_hi[:].bitcast(F32),
                                                ALU.subtract).then_inc(s["wlo_ok"], 1)
                        nc.vector.tensor_copy(sele_b[:], sele_f[:]).then_inc(s["sele_ok"], 1)

            dve.wait_ge(s["ld_x0"], 16)
            ln_stats(0, stats, mv, "stats_ok", "mv_ok")
            dve.wait_ge(s["modt_mm"], 1)
            nc.vector.tensor_copy(mod_t[:, 0:3:2, :],
                                  ps_s[0][:, 0:2 * NB].rearrange("p (m b) -> p m b", m=2)).then_inc(s["modt_ok"], 1)
            nc.vector.tensor_scalar(mod_t[:, 1:4:2, :], ps_s[0][:, 2 * NB:4 * NB].rearrange("p (m b) -> p m b", m=2),
                                    1.0, None, ALU.add).then_inc(s["modt_ok"], 1)
            dve.wait_ge(s["gate_mm"], 1)
            nc.vector.tensor_copy(gate8[:], ps_s[1][0:NB, 0:2 * D].rearrange("p (m d) -> p m d", m=2)).then_inc(s["gate8_a"], 1)
            dve.wait_ge(s["gate8_a"], 1)
            nc.vector.tensor_scalar(gate8s[:], gate8[:], 0.0, 2.0, ALU.is_ge, ALU.mult).then_inc(s["gate8_b"], 1)
            dve.wait_ge(s["gate8_b"], 1)
            nc.vector.tensor_scalar(gate8s[:], gate8s[:], -1.0, None, ALU.add).then_inc(s["gate8_b"], 1)
            dve.wait_ge(s["gate8_b"], 2)
            nc.vector.tensor_tensor(gate8m[:], gate8[:], gate8s[:], ALU.mult).then_inc(s["gate8_c"], 1)
            dve.wait_ge(s["gate8_c"], 1)
            nc.vector.scalar_tensor_tensor(gate8[:], gate8m[:], 0.25, gate8s[:], ALU.max, ALU.mult).then_inc(s["gate8_ok"], 1)
            ln_apply(0, mv, rstd, xn, "rstd_ok", "xn_ok")
            dve.wait_ge(s["ld_w2"], 16 * 9)
            nc.vector.tensor_scalar(nalpha[:], alpha_sb[:], -1.0, None, ALU.mult).then_inc(s["alpha_ok"], 1)
            nc.vector.tensor_copy(id_b[:], id_f[:]).then_inc(s["idb_ok"], 1)
            dve.wait_ge(s["decay_raw"], 1)
            nc.vector.tensor_scalar(decay[:], decay[:], float(HD) ** -0.5, None, ALU.mult).then_inc(s["decay_ok"], 1)
            qk_lo_of(0, 0)
            qk_lo_of(0, 1)
            v_bias(0, False)
            for h in range(4):
                dve.wait_ge(s["gateb_mm"], h + 1)
                nc.vector.tensor_copy(gates[:, 2 * h:2 * h + 2, :, :].rearrange("p b m d -> p (b m d)"),
                                      ps_o[h % 2][:] if h < 2 else ps_t[h % 2][:]).then_inc(s["gates_ok"], 1)
            dve.wait_ge(s["ld_x"], 16)
            dve.wait_ge(s["ld_late"], 16 * 6)
            dve.wait_ge(s["lg_init"], 1)
            dve.wait_ge(s["gates_ok"], 4)
            dve.wait_ge(s["decay_ok"], 1)
            chunk(0, True, False, True)
            with dve.Fori(1, NCHUNK - 1) as i:
                chunk(i, True, True, True)
            chunk(NCHUNK - 1, True, True, False)
            chunk(NCHUNK, False, True, False)

            nc.vector.memset(rz[:], 0.0).then_inc(s["act_ok"], FR)
            nc.vector.memset(zs[:], 0.0).then_inc(s["down_done"], FR)
            nc.vector.memset(rsum[:], 0.0).then_inc(s["y_free"], 1)
            with dve.Fori(0, NCHUNK) as i:
                for u in range(NU):
                    r = u % FR
                    shared = u == NU - 1
                    dve.wait_ge(s["silu_done"], i * NU + u + 1)
                    dve.wait_ge(s["up_done"], i * NU + u + 1)
                    dve.wait_ge(s["down_done"], i * NU + u + 1)
                    dst = act if shared else act_u
                    nc.vector.tensor_tensor(dst[:, r, :], act_g[:, r, :], ps_u[r][:],
                                            ALU.mult).then_inc(s["act_ok" if shared else "mul_done"], 1)
                    if not shared:
                        dve.wait_ge(s["mul_done"], i * (NU - 1) + u + 1)
                        dve.wait_ge(s["cb_done"], i * (NU - 1) + u + 1)
                        nc.vector.tensor_tensor(act[:, r, :], act_u[:, r, :], ps_c[:], ALU.mult).then_inc(s["act_ok"], 1)
                dve.wait_ge(s["down_done"], (i + 1) * NU + FR)
                gb = gates[:, bass.ds(i * BPC, BPC), 1, :].unsqueeze(2).to_broadcast([P, BPC, TT // BPC, D])
                nc.vector.tensor_tensor(mod2(res[:]), mod2(ps_y[:].rearrange("p (t d) -> p t d", t=TT)), gb,
                                        ALU.mult).then_inc(s["y_scaled"], 1)
                dve.wait_ge(s["y_scaled"], i + 1)
                xs = x_all[:, bass.ds(i * TT, TT), :]
                nc.vector.tensor_tensor(xs, xs, res[:], ALU.add).then_inc(s["y_free"], 1)

        @block.tensor
        def _(pe):
            def mm(o, l, r, start=True, stop=True, check=True, transpose=False):
                return nc.tensor.matmul(o, l, r, start=start, stop=stop, skip_group_check=not check,
                                        is_transpose=transpose or None)

            def transpose4(dst, src):
                for t in range(TT):
                    last = mm(dst[:, t * P:t * P + P], src[:, t, :], id_f[:], transpose=True)
                return last

            def lnt(c):
                pe.wait_ge(s["xn_ok"], c + 1)
                transpose4(ps_b, xn).then_inc(s["lnt_done"], 1)

            def project(c, i):
                pe.wait_ge(s["h_ok"], c + 1)
                if i == 1:
                    pe.wait_ge(s["qk_lo_ok"], c * 2 + 1)
                mm(ps_b[:], (wq_sb, wk_sb)[i][:], h_t[:]).then_inc(s["qk_mm"], 1)

            def project_v(c):
                for t in range(TT):
                    last = mm(ps_b[:, t * P:t * P + P], h_t[:, t * P:t * P + P], wv_sb[:])
                last.then_inc(s["v_mm"], 1)

            def scores(i, n, prev):
                g, b, j = n // 8, n // QUAD % BPC, n % QUAD
                if n % 8 == 0:
                    pe.wait_ge(s_st[g], (i + 1) * STACK)
                if prev or n >= 2:
                    pe.wait_ge(s["ttr_done"], i * STEPS + n - 1)
                rows = slice(32 * j, 32 * j + 32)
                for t in range(BPC):
                    q0 = b * SEQ + t * P
                    last = mm(ps_s[n % 2][:, t * SEQ:t * SEQ + SEQ], q_st[rows, g, q0:q0 + P],
                              k_st[rows, g, b * SEQ:b * SEQ + SEQ])
                last.then_inc(s["s_done"], 1)

            def turn(i, n, later):
                pe.wait_ge(s["nd_done"], i * STEPS + n + 1)
                if later or n >= 2:
                    pe.wait_ge(s["exp_done"], i * STEPS + n - 1)
                for kt in range(BPC):
                    for qt in range(BPC):
                        at = kt * SEQ + qt * P
                        last = mm(ps_t[n % 2][:, at:at + P], sc[:, n % RING, qt, kt * P:kt * P + P], id_f[:],
                                  transpose=True)
                last.then_inc(s["t_done"], 1)

            def values(i, q, later):
                g, b = q // BPC, q % BPC
                pe.wait_ge(s["exp_done"], i * STEPS + QUAD * q + QUAD)
                if b == 0:
                    pe.wait_ge(s["vgrp_ok"], i * NG + g + 1)
                    if later or g >= 2:
                        pe.wait_ge(s["ot_ok"], i * NG + g - 1)
                for kt in range(BPC):
                    for j in range(QUAD):
                        last = mm(ps_o[g % 2][VW * j:VW * j + VW, b * SEQ:b * SEQ + SEQ],
                                  v_one[:, b * BPC + kt, g, j, :], pr[:, (QUAD * q + j) % RING, kt, :],
                                  start=kt == 0, stop=kt == BPC - 1, check=False)
                last.then_inc(s["pv_done"], 1)

            def by_token(c, g):
                pe.wait_ge(s["ot_ok"], c * NG + g + 1)
                transpose4(ps_a, o_t[:, g % 2, :].rearrange("p (t k) -> p t k", t=TT)).then_inc(s["c_done"], 1)

            def chunk(i, cur, prev, nxt):
                for n in range(STEPS if cur else 24):
                    if cur:
                        scores(i, n, prev)
                    if n >= LAG_T and cur:
                        turn(i, n - LAG_T, prev)
                    elif n < LAG_T and prev:
                        turn(i - 1, n - LAG_T + STEPS, True)
                    if n % QUAD == 0:
                        if n >= LAG_PV and cur:
                            values(i, (n - LAG_PV) // QUAD, prev)
                        elif n < LAG_PV and prev:
                            values(i - 1, (n - LAG_PV + STEPS) // QUAD, True)
                    if n == 6 and prev:
                        pe.wait_ge(s["norm_ok"], i * NG - 1)
                        by_token(i - 1, 3)
                    if n == 8 and prev:
                        pe.wait_ge(s["norm_ok"], i * NG)
                        if cur:
                            pe.wait_ge(s["v_ok"], i + 1)
                        else:
                            pe.wait_ge(s["cwt_ok"], i - 1)
                        transpose4(ps_b, attn[:].rearrange("p t g j d -> p t (g j d)")).then_inc(s["at_done"], 1)
                    if n == 9 and nxt:
                        if prev:
                            pe.wait_ge(s["at_ok"], i)
                        else:
                            pe.wait_ge(s["v_ok"], 1)
                        lnt(i + 1)
                    if n == 10 and prev:
                        pe.wait_ge(s["at_ok"], i)
                        for t in range(TT):
                            last = mm(ps_a[:, t * P:t * P + P], attn_t[:, t * P:t * P + P], wo_sb[:])
                        last.then_inc(s["wo_done"], 1)
                    if n == 11 and nxt:
                        project(i + 1, 0)
                    if n == 13 and nxt:
                        project(i + 1, 1)
                    if n == 14 and prev:
                        pe.wait_ge(s["xn2_ok"], i)
                        transpose4(ps_a, xn2).then_inc(s["ln2t_done"], 1)
                    if n == 16 and prev:
                        pe.wait_ge(s["h2t_ok"], i)
                        pe.wait_ge(s["h2hi_ok"], i)
                        for t in range(TT):
                            last = mm(ps_a[:, t * E:t * E + E], h2_t[:, t * P:t * P + P], wr_sb[:])
                        last.then_inc(s["r_done"], 1)
                    if n == 18 and cur:
                        if prev:
                            pe.wait_ge(s["lg_ok"], i)
                        by_token(i, 0)
                    if n == 20 and prev:
                        if nxt:
                            pe.wait_ge(s["qk_lo_ok"], i * 2 + 4)
                        else:
                            pe.wait_ge(s["at_ok"], i)
                        pe.wait_ge(s["cp_ok"], i)
                        begin(pe, i)
                        for t in range(TT):
                            last = mm(ps_b[0:3 * E, t * P // 2:t * P // 2 + P // 2].bitcast(BF16),
                                      cwp[:, t, :, :].rearrange("p a e -> p (a e)"), id_b[:], transpose=True)
                        last.then_inc(s["cwt_done"], 1)
                    if n == 22 and nxt:
                        if prev:
                            pe.wait_ge(s["cwt_ok"], i)
                        else:
                            pe.wait_ge(s["qk_lo_ok"], i * 2 + 4)
                        project_v(i + 1)
                    if n in (24, 30) and cur:
                        g = {24: 1, 30: 2}[n]
                        pe.wait_ge(s["norm_ok"], i * NG + g)
                        by_token(i, g)

            pe.wait_ge(s["ld_w"], 48)
            pe.wait_ge(s["silu_ok"], 1)
            for k, m in enumerate((0, 3, 1, 4)):
                last = mm(ps_s[0][:, k * NB:k * NB + NB], wmod_sb[:, m, :], silu_c[:])
            last.then_inc(s["modt_mm"], 1)
            for k, m in enumerate((2, 5)):
                last = mm(ps_s[1][0:NB, k * D:k * D + D], silu_c[:], wmod_sb[:, m, :])
            last.then_inc(s["gate_mm"], 1)
            pe.wait_ge(s["gate8_ok"], 1)
            for h in range(4):
                dst = ps_o[h % 2] if h < 2 else ps_t[h % 2]
                for b in range(2):
                    last = mm(dst[:, b * 2 * D:b * 2 * D + 2 * D], selb_sb[:, 2 * h + b, :],
                              gate8[:].rearrange("p m d -> p (m d)"))
                last.then_inc(s["gateb_mm"], 1)
            pe.wait_ge(s["ld_w2"], 16 * 9)
            lnt(0)
            project(0, 0)
            project(0, 1)
            pe.wait_ge(s["qk_lo_ok"], 2)
            project_v(0)
            pe.wait_ge(s["gates_ok"], 4)
            pe.wait_ge(s["idb_ok"], 1)
            pe.wait_ge(s["ld_late"], 16 * 6)
            chunk(0, True, False, True)
            with pe.Fori(1, NCHUNK - 1) as i:
                chunk(i, True, True, True)
            chunk(NCHUNK - 1, True, True, False)
            chunk(NCHUNK, False, True, False)

            pe.wait_ge(s["cwt_ok"], NCHUNK)
            pe.wait_ge(s["h2lo_ok"], NCHUNK)
            pe.wait_ge(s["wlo_ok"], 1)
            pe.wait_ge(s["sele_ok"], 1)

            def part(i, u, half, dst, done):
                hi, lo = (a[:, bass.ds(i, 1), :].rearrange("p a n -> p (a n)") for a in (h2_hi, h2_lo))
                mm(dst[:], wgu_hi[:, u, half, :], hi, stop=False)
                mm(dst[:], wgu_lo[:, u, half, :], hi, start=False, stop=False)
                mm(dst[:], wgu_hi[:, u, half, :], lo, start=False).then_inc(s[done], 1)

            def down(i, u):
                if u == 0:
                    pe.wait_ge(s["y_free"], i + 1)
                pe.wait_ge(s["act_ok"], i * NU + u + 1 + FR)
                for t in range(TT):
                    last = mm(ps_y[:, t * D:t * D + D], act[:, u % FR, t * P:t * P + P], wd_sb[:, u, :],
                              start=u == 0 and t == 0, stop=u == NU - 1, check=False)
                last.then_inc(s["down_done"], 1)

            with pe.Fori(0, NCHUNK) as i:
                for u in range(NU):
                    pe.wait_ge(s["act_ok"], i * NU + u + 1)
                    part(i, u, 0, ps_g[u % FR], "gate_done")
                    part(i, u, 1, ps_u[u % FR], "up_done")
                    if u < NU - 1:
                        pe.wait_ge(s["act_ok"], i * NU + u + FR)
                        begin(pe, i)
                        mm(ps_c[:], sele_b[:, u, :],
                           cw_t[:, bass.ds(i, 1), :].rearrange("p a n -> p (a n)")).then_inc(s["cb_done"], 1)
                    if u:
                        down(i, u - 1)
                down(i, NU - 1)


_OUT = ("out_0_dram", (NB * SEQ, D))


def kernel(**inputs):
    import concourse.bacc as bacc
    from concourse.bass_utils import run_bass_kernel_spmd

    a = {k.replace("L0_attn_", "").replace("L0_ffn_", "").replace("L0_", ""): np.asarray(v)
         for k, v in inputs.items()}

    def by_unit(w, shared):
        w = w.reshape(E // 2, 2, D, FE).transpose(2, 0, 1, 3).reshape(D, E // 2, P)
        return np.concatenate([w, shared.reshape(D, 1, P)], axis=1)

    w_gu = np.stack([by_unit(a["Wg"], a["Sg"]), by_unit(a["Wu"], a["Su"])], axis=2)
    w_d = np.concatenate([a["Wd"].reshape(E // 2, P, D), a["Sd"].reshape(1, P, D)]).transpose(1, 0, 2)

    tok = np.arange(SEQ)
    lag = np.abs(tok[:, None] - tok[None, :]).astype(np.float32).reshape(BPC, P, SEQ).transpose(1, 0, 2)
    ident = np.eye(P, dtype=np.float32)
    sel_b = np.repeat(np.eye(NB, dtype=np.float32)[:, :, None], P, axis=2)
    sel_e = np.zeros((3, E, NU - 1, P), np.float32)
    for e in range(E):
        sel_e[:, e, e // 2, (e % 2) * FE:(e % 2) * FE + FE] = 1.0

    arrays = {
        "x": a["x"].reshape(NB * SEQ, D), "c_t": a["c"].T, "wq_t": a["Wq"].T, "wk_t": a["Wk"].T,
        "wv_t": a["Wv"].T, "wo_t": a["Wo"].T, "b_q": a["bq"].reshape(D, 1), "b_k": a["bk"].reshape(D, 1),
        "b_v": a["bv"].reshape(1, D), "b_o": a["bo"].reshape(1, D), "alpha": a["alpha"].reshape(1, 1),
        "w_r": a["Wr"], "w_gu": w_gu, "w_d": w_d, "w_mod": a["wmod"].reshape(D, 6, D),
        "lag": lag, "ident": ident, "sel_b": sel_b, "sel_e": sel_e.reshape(3 * E, NU - 1, P),
    }
    arrays = {f"in_{k}": np.ascontiguousarray(v) for k, v in arrays.items()}
    nc = bacc.Bacc("TRN2", target_bir_lowering=False, num_devices=1)
    args = [nc.dram_tensor(k, v.shape, mybir.dt.from_np(v.dtype), kind="ExternalInput").ap()
            for k, v in arrays.items()]
    args.append(nc.dram_tensor(_OUT[0], _OUT[1], F32, kind="ExternalOutput").ap())
    build(nc, *args)
    r = run_bass_kernel_spmd(nc, [arrays], core_ids=[0])
    return r.results[0][_OUT[0]].reshape(NB, SEQ, D)
```

```python
from contextlib import ExitStack

import numpy as np

import concourse.bass as bass
from concourse import mybir

F32 = mybir.dt.float32
F32R = mybir.dt.float32r
BF16 = mybir.dt.bfloat16
ALU = mybir.AluOpType
ACT = mybir.ActivationFunctionType
AX_X = mybir.AxisListType.X

P = 128
NB, SEQ, D = 8, 256, 128
HEADS, HD = 16, 8
E, FE, FS = 16, 64, 128
EPS = 1e-5
CHUNK = 512
NCHUNK = NB * SEQ // CHUNK
TT = CHUNK // P
BPC = CHUNK // SEQ
QUAD = 4
NG = HEADS // QUAD
STEPS = BPC * HEADS
QUADS = STEPS // QUAD
SLOTS = 4
VW = 32
NU = E * FE // P + FS // P
ROUTED = NU - 1
STACK = SLOTS * 16
RING = 8
SB = 3
FR = 3
LAG_T, LAG_PV = 4, 9
LAG_D = 2
NEG = -3.0e38
Q_HI, Q_LO, K_LO, K_HI = range(4)
SLOT_BLOCKS = ((Q_HI, K_HI), (Q_HI, K_LO), (Q_LO, K_HI), (Q_LO, K_LO))
W_Q, W_K, W_V, W_O = range(4)
B_Q, B_K, B_V, B_O = range(4)
SA, CA1, SB_, CB1, GA, GB = range(6)


def score_bank(n):
    return n % SB


def score_bank_before(n):
    return max(m for m in range(-STEPS, n) if (m % STEPS) % SB == n % SB)


def build(nc, x, c_t, w_attn, vecs, alpha, w_r, w_gu, w_d, w_mod, lag, ident, sel_e, out):
    x_v = x.rearrange("(n p) d -> p n d", p=P)
    out_v = out.rearrange("(n p) d -> p n d", p=P)

    with ExitStack() as ctx:
        def sb(name, shape, dt=F32):
            return ctx.enter_context(nc.sbuf_tensor(name, shape, dt))

        def sem(name):
            return ctx.enter_context(nc.semaphore(name))

        id_f = sb("id_f", [P, P])
        id_b = sb("id_b", [P, P], BF16)
        decay = sb("decay", [P, BPC, SEQ])
        alpha_sb, nalpha = sb("alpha_sb", [P, 1]), sb("nalpha", [P, 1])
        wa_sb = sb("wa_sb", [P, 4, D])
        vec_sb = sb("vec_sb", [P, 4])
        wr_sb = sb("wr_sb", [P, E])
        wgu_sb = sb("wgu_sb", [P, NU, 2, P])
        wgu_hi = sb("wgu_hi", [P, NU, 2, P], F32R)
        wgu_lo = sb("wgu_lo", [P, NU, 2, P], F32R)
        wd_sb = sb("wd_sb", [P, NU, D])
        wd_hi = sb("wd_hi", [P, NU, D], F32R)
        wd_lo = sb("wd_lo", [P, NU, D], F32R)
        wmod_sb = sb("wmod_sb", [P, 6, D])
        sele_f = sb("sele_f", [3 * E, ROUTED, P])
        sele_b = sb("sele_b", [3 * E, ROUTED, P], BF16)
        ct_sb, silu_c = sb("ct_sb", [P, NB]), sb("silu_c", [P, NB])
        mod_t = sb("mod_t", [P, 6, NB])
        gate_s, gate_m = sb("gate_s", [P, 2, NB]), sb("gate_m", [P, 2, NB])
        bo2, ga_bo = sb("bo2", [P, 1]), sb("ga_bo", [P, NB])
        nhalf = sb("nhalf", [P, TT])
        x_all = sb("x_all", [P, NCHUNK * TT, D])
        stats, mv, var_e, rstd = (sb("stats", [P, TT, 6]), sb("mv", [P, TT, 2]),
                                  sb("var_e", [P, TT]), sb("rstd", [P, TT]))
        stats2, mv2, var_e2, rstd2 = (sb("stats2", [P, TT, 6]), sb("mv2", [P, TT, 2]),
                                      sb("var_e2", [P, TT]), sb("rstd2", [P, TT]))
        xn, xn2 = sb("xn", [P, TT, D]), sb("xn2", [P, TT, D])
        h_t, h2_t = sb("h_t", [P, CHUNK]), sb("h2_t", [P, CHUNK])
        h2_hi = sb("h2_hi", [P, NCHUNK, CHUNK], F32R)
        h2_lo = sb("h2_lo", [P, NCHUNK, CHUNK], F32R)
        qk = sb("qk", [P, 4, CHUNK], F32R)
        qk_st = sb("qk_st", [P, 2, NG, CHUNK], F32R)
        v_nat = sb("v_nat", [P, TT, NG, QUAD, HD])
        v_one = sb("v_one", [P, TT, NG, QUAD, VW])
        sc = sb("sc", [P, RING, BPC, SEQ])
        mx = sb("mx", [P, RING, BPC])
        pr = sb("pr", [P, RING, BPC, SEQ])
        o_t = sb("o_t", [P, 2, CHUNK])
        rsum = sb("rsum", [P, TT, QUAD])
        attn = sb("attn", [P, TT, NG, QUAD, HD])
        attn_t, res_t = sb("attn_t", [P, CHUNK]), sb("res_t", [P, CHUNK])
        lg = sb("lg", [P, TT, E + 8])
        top8 = sb("top8", [P, TT, 8])
        struck = sb("struck", [P, TT, E + 8])
        ex, rz, zs = sb("ex", [P, TT, E]), sb("rz", [P, TT]), sb("zs", [P, TT])
        cw = sb("cw", [P, TT, E])
        cwp = sb("cwp", [P, TT, 3, E], BF16)
        cw_t = sb("cw_t", [3 * E, NCHUNK, CHUNK], BF16)
        act_g = sb("act_g", [P, FR, CHUNK])
        act_u = sb("act_u", [P, FR, CHUNK])
        act = sb("act", [P, FR, CHUNK])
        act_hi = sb("act_hi", [P, FR, CHUNK], F32R)
        act_lo = sb("act_lo", [P, FR, CHUNK], F32R)
        y_t = sb("y_t", [P, CHUNK])

        bank = [ctx.enter_context(nc.psum_tensor(f"bank{i}", [P, CHUNK], F32)) for i in range(8)]
        ps_s, ps_t, ps_o, ps_a, ps_b = bank[0:SB], bank[3:5], bank[5], bank[6], bank[7]
        ps_gu, ps_c, ps_y, ps_x = bank[0:FR], bank[3], bank[4], bank[5]

        s = {n: sem(n) for n in (
            "ld_x0 ld_x ld_mod ld_attn ld_decay ld_ffn nalpha_ok decay_raw decay_ok silu_ok modt_mm modt_ok "
            "bo_mm bo_ok gate_a gate_b gate_c gate_ok gabo_ok idb_ok vone_ok pool_init lg_init whi_ok wlo_ok "
            "sele_ok stats_ok mv_ok vare_ok rstd_ok xn_ok lnt_done h_ok qk_mm qk_hi_ok qk_lo_ok v_mm v_ok "
            "vgrp_ok s_done ttr_done nd_done t_done exp_done pv_done ot_ok c_done rs_ok norm_ok "
            "at_done at_ok wo_done rt_ok rx_done x2_ok stats2_ok mv2_ok vare2_ok rstd2_ok xn2_ok ln2t_done "
            "h2t_ok h2hi_ok h2lo_ok r_done lg_ok top_ok fill_ok ls_ok struck_ok ex_ok zs_ok rz_ok em_ok "
            "cw_ok cp0_ok cp1_ok r1_ok cp_ok cwt_done cwt_ok "
            "gate_done up_done cb_done silu_done mul_done act_ok ahi_ok alo_ok down_done yt_ok yx_done "
            "y_added").split()}
        s_st = [sem(f"stacked{g}") for g in range(NG)]
        s_out = sem("out_written")
        begun = {e: sem(f"begun{k}") for k, e in enumerate((nc.vector, nc.gpsimd, nc.tensor, nc.scalar))}

        block = ctx.enter_context(nc.Block())

        def begin(eng, i):
            if not isinstance(i, int):
                eng.sem_inc(begun[eng])

        def of_chunk(ap, c, r=slice(None)):
            return ap[:, bass.ds(c, 1), r].rearrange("p a n -> p (a n)")

        def seq_cols(b):
            return slice(b * SEQ, b * SEQ + SEQ)

        @block.sync
        def _(sp):
            sp.dma_start(x_all[:, 0:TT, :], x_v[:, 0:TT, :]).then_inc(s["ld_x0"], 16)
            for ap, dram in ((ct_sb[:], c_t), (wmod_sb[:], w_mod)):
                sp.dma_start(ap, dram).then_inc(s["ld_mod"], 16)
            for ap, dram in ((id_f[:], ident), (wa_sb[:], w_attn), (vec_sb[:], vecs)):
                sp.dma_start(ap, dram).then_inc(s["ld_attn"], 16)
            for ap, dram in ((decay[:], lag), (alpha_sb[:], alpha.to_broadcast([P, 1]))):
                sp.dma_start(ap, dram).then_inc(s["ld_decay"], 16)
            sp.dma_start(x_all[:, TT:, :], x_v[:, TT:, :]).then_inc(s["ld_x"], 16)
            for ap, dram in ((wr_sb[:], w_r), (sele_f[:], sel_e), (wgu_sb[:], w_gu), (wd_sb[:], w_d)):
                sp.dma_start(ap, dram).then_inc(s["ld_ffn"], 16)

            def stack(c, g, reused):
                if g == 0 or not reused:
                    sp.wait_ge(s["qk_lo_ok"], c * 2 + 2)
                if reused:
                    sp.wait_ge(s["s_done"], (c - 1) * STEPS + 8 * g + 8)
                for slot, (bq, bk) in enumerate(SLOT_BLOCKS):
                    sp.dma_start(qk_st[slot:P:SLOTS, :, g, :].bitcast(F32),
                                 qk[32 * g:32 * g + 32, bq:bk + 1:bk - bq, :].bitcast(F32)).then_inc(s_st[g], 16)

            def chunk(i, nxt, first=False):
                stack(i, 3, reused=not first)
                if nxt:
                    for g in range(3):
                        stack(i + 1, g, reused=True)

            for g in range(3):
                stack(0, g, reused=False)
            chunk(0, True, first=True)
            with sp.Fori(1, NCHUNK - 1) as i:
                chunk(i, True)
            chunk(NCHUNK - 1, False)

            with sp.Fori(0, NCHUNK) as i:
                sp.wait_ge(s["y_added"], i + 1)
                sp.dma_start(out_v[:, bass.ds(i * TT, TT), :],
                             x_all[:, bass.ds(i * TT, TT), :]).then_inc(s_out, 16)
            sp.wait_ge(s_out, 16 * NCHUNK)

        @block.gpsimd
        def _(pool):
            nc.gpsimd.memset(nhalf[:], -0.5).then_inc(s["pool_init"], 1)
            nc.gpsimd.memset(lg[:], NEG).then_inc(s["lg_init"], 1)

            def rstd_of(c, mv_, var_, rstd_, ready, mid, done):
                pool.wait_ge(s[ready], c + 1)
                begin(pool, c)
                nc.gpsimd.tensor_scalar(var_[:], mv_[:, :, 1], 1.0, EPS, ALU.mult, ALU.add).then_inc(s[mid], 1)
                pool.wait_ge(s[mid], c + 1)
                nc.gpsimd.tensor_tensor(rstd_[:], var_[:], nhalf[:], ALU.pow).then_inc(s[done], 1)

            def ln1(c):
                rstd_of(c, mv, var_e, rstd, "mv_ok", "vare_ok", "rstd_ok")

            def ln2(c):
                rstd_of(c, mv2, var_e2, rstd2, "mv2_ok", "vare2_ok", "rstd2_ok")

            def chunk(i, prev, nxt):
                for n in range(STEPS):
                    pool.wait_ge(s["ttr_done"], i * STEPS + n + 1)
                    begin(pool, i)
                    for t in range(BPC):
                        last = nc.gpsimd.tensor_scalar(sc[:, n % RING, t, :], sc[:, n % RING, t, :], -1.0,
                                                       mx[:, n % RING, t:t + 1], ALU.mult, ALU.add)
                    last.then_inc(s["nd_done"], 1)
                    if n == 4 and nxt:
                        ln1(i + 1)
                    if n == 15 and prev:
                        ln2(i - 1)

            pool.wait_ge(s["pool_init"], 1)
            ln1(0)
            nc.gpsimd.memset(v_one[:], 0.0).then_inc(s["pool_init"], 1)
            pool.wait_ge(s["pool_init"], 2)
            nc.gpsimd.memset(v_one[:, :, :, :, HD:HD + 1], 1.0).then_inc(s["vone_ok"], 1)
            pool.wait_ge(s["ld_attn"], 48)
            nc.gpsimd.tensor_copy(id_b[:], id_f[:]).then_inc(s["idb_ok"], 1)
            pool.wait_ge(s["ld_ffn"], 64)
            nc.gpsimd.tensor_copy(sele_b[:], sele_f[:]).then_inc(s["sele_ok"], 1)
            chunk(0, False, True)
            with pool.Fori(1, NCHUNK - 1) as i:
                chunk(i, True, True)
            chunk(NCHUNK - 1, True, False)

            def ffn(i, tail):
                for u in range(NU):
                    pool.wait_ge(s["ahi_ok"], i * NU + u + 1)
                    nc.gpsimd.tensor_tensor(act_lo[:, u % FR, :], act[:, u % FR, :],
                                            act_hi[:, u % FR, :].bitcast(F32), ALU.subtract).then_inc(s["alo_ok"], 1)
                    if tail and u == 4:
                        ln2(NCHUNK - 1)

            ffn(0, True)
            with pool.Fori(1, NCHUNK) as i:
                ffn(i, False)

        @block.scalar
        def _(act_e):
            def affine(dst, src, at, scale, bias):
                return nc.scalar.activation(dst, src, ACT.Identity, bias=bias[:, bass.ds(at, 1)],
                                            scale=scale[:, bass.ds(at, 1)])

            def h1(c):
                act_e.wait_ge(s["lnt_done"], c + 1)
                for b in range(BPC):
                    last = affine(h_t[:, seq_cols(b)], ps_b[:, seq_cols(b)], c * BPC + b,
                                  mod_t[:, CA1, :], mod_t[:, SA, :])
                last.then_inc(s["h_ok"], 1)

            def qk_hi_of(c, i, reused, ps=ps_b):
                act_e.wait_ge(s["qk_mm"], c * 2 + i + 1)
                if reused and i == 0:
                    act_e.wait_ge(s_st[NG - 1], c * STACK)
                nc.scalar.activation(qk[:, (Q_HI, K_HI)[i], :], ps[:], ACT.Identity,
                                     bias=vec_sb[:, (B_Q, B_K)[i]:(B_Q, B_K)[i] + 1],
                                     scale=1.0).then_inc(s["qk_hi_ok"], 1)

            def v_take(c):
                act_e.wait_ge(s["v_mm"], c + 1)
                nc.scalar.activation(v_nat[:].rearrange("p t g j d -> p (t g j d)"), ps_b[:],
                                     ACT.Copy).then_inc(s["v_ok"], 1)

            def v_group(c, g, reused):
                act_e.wait_ge(s["v_ok"], c + 1)
                if reused:
                    act_e.wait_ge(s["pv_done"], (c - 1) * QUADS + 2 * g + 2)
                nc.scalar.activation(v_one[:, :, g, :, 0:HD], v_nat[:, :, g, :, :],
                                     ACT.Copy).then_inc(s["vgrp_ok"], 1)

            def out_t(c, g, first):
                act_e.wait_ge(s["pv_done"], c * QUADS + 2 * g + 2)
                if not (first and g < 2):
                    act_e.wait_ge(s["c_done"], c * NG + g - 1)
                nc.scalar.activation(o_t[:, g % 2, :], ps_o[:], ACT.Copy).then_inc(s["ot_ok"], 1)

            def exps(i, m, later):
                act_e.wait_ge(s["t_done"], i * STEPS + m + 1)
                if m % QUAD == 0 and (later or m >= RING):
                    act_e.wait_ge(s["pv_done"], i * QUADS + m // QUAD - 1)
                nc.scalar.activation(pr[:, m % RING, :, :].rearrange("p a b -> p (a b)"), ps_t[m % 2][:],
                                     ACT.Exp, scale=-1.0).then_inc(s["exp_done"], 1)

            def attn_take(c):
                act_e.wait_ge(s["at_done"], c + 1)
                nc.scalar.activation(attn_t[:], ps_b[:], ACT.Copy).then_inc(s["at_ok"], 1)

            def gated(c):
                act_e.wait_ge(s["wo_done"], c + 1)
                for b in range(BPC):
                    last = affine(res_t[:, seq_cols(b)], ps_a[:, seq_cols(b)], c * BPC + b, mod_t[:, GA, :], ga_bo)
                last.then_inc(s["rt_ok"], 1)

            def h2(c):
                act_e.wait_ge(s["ln2t_done"], c + 1)
                for dst, done in ((h2_t[:], "h2t_ok"), (of_chunk(h2_hi, c), "h2hi_ok")):
                    for b in range(BPC):
                        last = affine(dst[:, seq_cols(b)], ps_a[:, seq_cols(b)], c * BPC + b,
                                      mod_t[:, CB1, :], mod_t[:, SB_, :])
                    last.then_inc(s[done], 1)

            def router_exp(c):
                act_e.wait_ge(s["ls_ok"], c + 1)
                nc.scalar.activation(ex[:], ex[:], ACT.Exp).then_inc(s["ex_ok"], 1)

            def weights_take(c):
                act_e.wait_ge(s["cwt_done"], c + 1)
                nc.scalar.activation(of_chunk(cw_t, c), ps_b[0:3 * E, 0:CHUNK // 2].bitcast(BF16),
                                     ACT.Copy).then_inc(s["cwt_ok"], 1)

            def chunk(i, prev, nxt):
                for n in range(STEPS):
                    if n >= LAG_T:
                        exps(i, n - LAG_T, prev)
                    elif prev:
                        exps(i - 1, n - LAG_T + STEPS, True)
                    if n == 2 and not prev:
                        v_take(i)
                    if n in (3, 4, 5, 7) and not prev:
                        v_group(i, {3: 0, 4: 1, 5: 2, 7: 3}[n], False)
                    if n == 1 and prev:
                        v_group(i, 2, True)
                    if n == 6 and prev:
                        out_t(i - 1, 3, False)
                    if n == 8 and prev:
                        v_group(i, 3, True)
                    if n == 10 and prev:
                        attn_take(i - 1)
                    if n == 12 and prev:
                        gated(i - 1)
                    if n == 13 and nxt:
                        h1(i + 1)
                    if n in (14, 22, 30):
                        out_t(i, (n - 14) // 8, not prev)
                    if n == 15 and nxt:
                        qk_hi_of(i + 1, 0, True)
                    if n == 18 and nxt:
                        qk_hi_of(i + 1, 1, True)
                    if n == 19 and prev:
                        h2(i - 1)
                    if n == 21 and nxt:
                        v_take(i + 1)
                    if n in (22, 24) and nxt:
                        v_group(i + 1, {22: 0, 24: 1}[n], True)
                    if n == 25 and prev:
                        router_exp(i - 1)
                    if n == 31 and prev:
                        weights_take(i - 1)
                    if 8 <= n < 8 + 2 * NU and n % 2 == 0 and not prev:
                        u = (n - 8) // 2
                        if u == 0:
                            act_e.wait_ge(s["ld_ffn"], 64)
                        nc.scalar.activation(wgu_hi[:, u, :, :], wgu_sb[:, u, :, :], ACT.Copy)
                        nc.scalar.activation(wd_hi[:, u, :], wd_sb[:, u, :], ACT.Copy).then_inc(s["whi_ok"], 1)

            act_e.wait_ge(s["ld_mod"], 32)
            nc.scalar.activation(silu_c[:], ct_sb[:], ACT.Silu).then_inc(s["silu_ok"], 1)
            act_e.wait_ge(s["ld_decay"], 32)
            act_e.wait_ge(s["nalpha_ok"], 1)
            nc.scalar.activation(decay[:], decay[:], ACT.Exp, scale=nalpha[:, 0:1]).then_inc(s["decay_raw"], 1)
            act_e.wait_ge(s["modt_ok"], 2)
            h1(0)
            qk_hi_of(0, 0, False)
            qk_hi_of(0, 1, False, ps_a)
            act_e.wait_ge(s["vone_ok"], 1)
            act_e.wait_ge(s["gabo_ok"], 1)
            chunk(0, False, True)
            with act_e.Fori(1, NCHUNK - 1) as i:
                chunk(i, True, True)
            chunk(NCHUNK - 1, True, False)
            for m in range(STEPS - LAG_T, STEPS):
                exps(NCHUNK - 1, m, True)

            def upper(i, u, first=False):
                act_e.wait_ge(s["act_ok"], i * NU + u + 1)
                if not (first and u < FR):
                    act_e.wait_ge(s["down_done"], i * NU + u + 1 - FR)
                nc.scalar.activation(act_hi[:, u % FR, :], act[:, u % FR, :], ACT.Copy).then_inc(s["ahi_ok"], 1)

            def y_gated(c):
                act_e.wait_ge(s["down_done"], c * NU + NU)
                for b in range(BPC):
                    last = nc.scalar.activation(y_t[:, seq_cols(b)], ps_y[:, seq_cols(b)], ACT.Identity,
                                                scale=mod_t[:, GB, bass.ds(c * BPC + b, 1)])
                last.then_inc(s["yt_ok"], 1)

            def ffn(i, tail):
                for u in range(NU):
                    act_e.wait_ge(s["gate_done"], i * NU + u + 1)
                    nc.scalar.activation(act_g[:, u % FR, :], ps_gu[2 * u % FR][:],
                                         ACT.Silu).then_inc(s["silu_done"], 1)
                    if u:
                        upper(i, u - 1, tail)
                    elif not tail:
                        upper(i - 1, NU - 1)
                    if u == 1 and not tail:
                        y_gated(i - 1)
                    if tail:
                        c = NCHUNK - 1
                        if u == 0:
                            out_t(c, 3, False)
                        if u == 2:
                            attn_take(c)
                        if u == 3:
                            gated(c)
                        if u == 6:
                            h2(c)
                        if u == 7:
                            router_exp(c)
                if tail:
                    weights_take(NCHUNK - 1)

            ffn(0, True)
            with act_e.Fori(1, NCHUNK) as i:
                ffn(i, False)
            upper(NCHUNK - 1, NU - 1)
            y_gated(NCHUNK - 1)

        @block.vector
        def _(dve):
            def tile_of(c, t):
                return x_all[:, bass.ds(c * TT + t, 1), :].rearrange("p a d -> p (a d)")

            def ln_stats(c, st, sem_st):
                begin(dve, c)
                for t in range(TT):
                    last = nc.vector.bn_stats(st[:, t, :], tile_of(c, t))
                last.then_inc(s[sem_st], 1)

            def ln_mean(c, st, mv_, sem_st, sem_mv):
                dve.wait_ge(s[sem_st], c + 1)
                begin(dve, c)
                for t in range(TT):
                    last = nc.vector.bn_aggr(mv_[:, t, :], st[:, t, :])
                last.then_inc(s[sem_mv], 1)

            def ln_apply(c, mv_, rstd_, dst, sem_r, sem_x):
                dve.wait_ge(s[sem_r], c + 1)
                for t in range(TT):
                    last = nc.vector.tensor_scalar(dst[:, t, :], tile_of(c, t), mv_[:, t, 0:1], rstd_[:, t:t + 1],
                                                   ALU.subtract, ALU.mult)
                last.then_inc(s[sem_x], 1)

            def qk_lo_of(c, i, ps=ps_b):
                dve.wait_ge(s["qk_hi_ok"], c * 2 + i + 1)
                bias = vec_sb[:, (B_Q, B_K)[i]:(B_Q, B_K)[i] + 1]
                nc.vector.scalar_tensor_tensor(qk[:, (Q_LO, K_LO)[i], :], ps[:], bias,
                                               qk[:, (Q_HI, K_HI)[i], :].bitcast(F32), ALU.add,
                                               ALU.subtract).then_inc(s["qk_lo_ok"], 1)

            def norm(c, g, first):
                src = ps_a[:].rearrange("p (t j w) -> p t j w", t=TT, j=QUAD)
                dve.wait_ge(s["c_done"], c * NG + g + 1)
                nc.vector.reciprocal(rsum[:], src[:, :, :, HD]).then_inc(s["rs_ok"], 1)
                dve.wait_ge(s["rs_ok"], c * NG + g + 1)
                if g == 0 and not first:
                    dve.wait_ge(s["at_done"], c)
                nc.vector.tensor_tensor(attn[:, :, g, :, :], src[:, :, :, 0:HD],
                                        rsum[:].unsqueeze(3).to_broadcast([P, TT, QUAD, HD]),
                                        ALU.mult).then_inc(s["norm_ok"], 1)

            def residual(c):
                dve.wait_ge(s["rx_done"], c + 1)
                xs = x_all[:, bass.ds(c * TT, TT), :]
                nc.vector.tensor_tensor(xs, xs, ps_a[:].rearrange("p (t d) -> p t d", t=TT),
                                        ALU.add).then_inc(s["x2_ok"], 1)
                dve.wait_ge(s["x2_ok"], c + 1)

            def h2_lo_of(c):
                dve.wait_ge(s["h2hi_ok"], c + 1)
                nc.vector.tensor_tensor(of_chunk(h2_lo, c), h2_t[:], of_chunk(h2_hi, c).bitcast(F32),
                                        ALU.subtract).then_inc(s["h2lo_ok"], 1)

            def r_take(c):
                dve.wait_ge(s["r_done"], c + 1)
                nc.vector.tensor_copy(lg[:, :, 0:E],
                                      ps_a[:, 0:TT * E].rearrange("p (t e) -> p t e", t=TT)).then_inc(s["lg_ok"], 1)

            def r_top(c):
                dve.wait_ge(s["lg_ok"], c + 1)
                begin(dve, c)
                for t in range(TT):
                    last = nc.vector.max(top8[:, t, :], lg[:, t, 0:E])
                last.then_inc(s["top_ok"], 1)

            def r_shift(c):
                dve.wait_ge(s["top_ok"], c + 1)
                nc.vector.tensor_tensor(ex[:], lg[:, :, 0:E], top8[:, :, 0:1].to_broadcast([P, TT, E]),
                                        ALU.subtract).then_inc(s["ls_ok"], 1)

            def r_fill(c):
                dve.wait_ge(s["top_ok"], c + 1)
                nc.vector.memset(top8[:, :, 2:8], NEG).then_inc(s["fill_ok"], 1)

            def r_strike(c):
                dve.wait_ge(s["fill_ok"], c + 1)
                begin(dve, c)
                for t in range(TT):
                    last = nc.vector.match_replace(struck[:, t, :], top8[:, t, :], lg[:, t, :], 3.0e38)
                last.then_inc(s["struck_ok"], 1)

            def r_sum(c):
                dve.wait_ge(s["ex_ok"], c + 1)
                nc.vector.tensor_reduce(zs[:], ex[:], AX_X, ALU.add).then_inc(s["zs_ok"], 1)

            def r_mask(c):
                dve.wait_ge(s["struck_ok"], c + 1)
                nc.vector.tensor_tensor(cw[:], struck[:, :, 0:E], lg[:, :, 0:E], ALU.not_equal).then_inc(s["em_ok"], 1)

            def r_inverse(c):
                dve.wait_ge(s["zs_ok"], c + 1)
                nc.vector.reciprocal(rz[:], zs[:]).then_inc(s["rz_ok"], 1)

            def r_keep(c):
                dve.wait_ge(s["em_ok"], 2 * c + 1)
                nc.vector.tensor_tensor(cw[:], cw[:], ex[:], ALU.mult).then_inc(s["em_ok"], 1)

            def r_weight(c):
                dve.wait_ge(s["em_ok"], 2 * c + 2)
                dve.wait_ge(s["rz_ok"], c + 1)
                nc.vector.tensor_tensor(cw[:], cw[:], rz[:].unsqueeze(2).to_broadcast([P, TT, E]),
                                        ALU.mult).then_inc(s["cw_ok"], 1)

            def r_part0(c):
                dve.wait_ge(s["cw_ok"], c + 1)
                nc.vector.tensor_copy(cwp[:, :, 0, :], cw[:]).then_inc(s["cp0_ok"], 1)

            def r_rest(c):
                dve.wait_ge(s["cp0_ok"], c + 1)
                nc.vector.tensor_tensor(cw[:], cw[:], cwp[:, :, 0, :], ALU.subtract).then_inc(s["r1_ok"], 1)

            def r_part1(c):
                dve.wait_ge(s["r1_ok"], c + 1)
                nc.vector.tensor_copy(cwp[:, :, 1, :], cw[:]).then_inc(s["cp1_ok"], 1)

            def r_part2(c):
                dve.wait_ge(s["cp1_ok"], c + 1)
                nc.vector.tensor_tensor(cwp[:, :, 2, :], cw[:], cwp[:, :, 1, :], ALU.subtract).then_inc(s["cp_ok"], 1)

            def step(i, n, prev, between=None, after=None):
                dve.wait_ge(s["s_done"], i * STEPS + n + 1)
                if prev or n >= RING:
                    dve.wait_ge(s["t_done"], i * STEPS + n - RING + 1)
                begin(dve, i)
                for t, side in ((0, between), (1, after)):
                    last = nc.vector.tensor_tensor_reduce(
                        sc[:, n % RING, t, :], ps_s[score_bank(n)][:, t * SEQ:t * SEQ + SEQ], decay[:, t, :],
                        1.0, NEG, ALU.mult, ALU.max, mx[:, n % RING, t:t + 1])
                    if t == 1:
                        last.then_inc(s["ttr_done"], 1)
                    if side and prev:
                        side(i - 1)

            stages = {22: (r_take, r_top), 23: (r_shift, r_fill), 24: (r_strike, None), 26: (r_sum, r_mask),
                      27: (r_inverse, r_keep), 28: (r_weight, r_part0), 29: (r_rest, r_part1), 30: (r_part2, None)}

            def chunk(i, prev, nxt):
                for n in range(STEPS):
                    step(i, n, prev, *stages.get(n, (None, None)))
                    if n == 0 and prev:
                        norm(i - 1, 2, False)
                    if n == 3 and nxt:
                        if not prev:
                            dve.wait_ge(s["ld_x"], 16)
                        ln_stats(i + 1, stats, "stats_ok")
                    if n == 4 and nxt:
                        ln_mean(i + 1, stats, mv, "stats_ok", "mv_ok")
                    if n == 8 and prev:
                        norm(i - 1, 3, False)
                    if n == 9 and nxt:
                        ln_apply(i + 1, mv, rstd, xn, "rstd_ok", "xn_ok")
                    if n == 14 and prev:
                        residual(i - 1)
                        ln_stats(i - 1, stats2, "stats2_ok")
                    if n == 15 and prev:
                        ln_mean(i - 1, stats2, mv2, "stats2_ok", "mv2_ok")
                    if n == 16:
                        norm(i, 0, not prev)
                    if n == 16 and nxt:
                        qk_lo_of(i + 1, 0)
                    if n == 17 and prev:
                        ln_apply(i - 1, mv2, rstd2, xn2, "rstd2_ok", "xn2_ok")
                    if n == 19 and nxt:
                        qk_lo_of(i + 1, 1)
                    if n == 21 and prev:
                        h2_lo_of(i - 1)
                    if n == 24:
                        norm(i, 1, not prev)
                    if 9 <= n < 9 + 2 * NU and n % 2 == 1 and not prev:
                        u = (n - 9) // 2
                        dve.wait_ge(s["whi_ok"], u + 1)
                        nc.vector.tensor_tensor(wgu_lo[:, u, :, :], wgu_sb[:, u, :, :],
                                                wgu_hi[:, u, :, :].bitcast(F32), ALU.subtract)
                        nc.vector.tensor_tensor(wd_lo[:, u, :], wd_sb[:, u, :], wd_hi[:, u, :].bitcast(F32),
                                                ALU.subtract).then_inc(s["wlo_ok"], 1)

            dve.wait_ge(s["ld_x0"], 16)
            ln_stats(0, stats, "stats_ok")
            ln_mean(0, stats, mv, "stats_ok", "mv_ok")
            dve.wait_ge(s["ld_decay"], 32)
            nc.vector.tensor_scalar(nalpha[:], alpha_sb[:], -1.0, None, ALU.mult).then_inc(s["nalpha_ok"], 1)
            dve.wait_ge(s["modt_mm"], 1)
            nc.vector.tensor_copy(mod_t[:, SA:SB_ + 1:SB_ - SA, :],
                                  ps_s[0][:, 0:2 * NB].rearrange("p (m b) -> p m b", m=2)).then_inc(s["modt_ok"], 1)
            nc.vector.tensor_scalar(mod_t[:, CA1:CB1 + 1:CB1 - CA1, :],
                                    ps_s[0][:, 2 * NB:4 * NB].rearrange("p (m b) -> p m b", m=2),
                                    1.0, None, ALU.add).then_inc(s["modt_ok"], 1)
            ln_apply(0, mv, rstd, xn, "rstd_ok", "xn_ok")
            gate = mod_t[:, GA:GB + 1, :]
            nc.vector.tensor_copy(gate, ps_s[0][:, 4 * NB:6 * NB].rearrange("p (m b) -> p m b", m=2)).then_inc(s["gate_a"], 1)
            dve.wait_ge(s["gate_a"], 1)
            nc.vector.tensor_scalar(gate_s[:], gate, 0.0, 2.0, ALU.is_ge, ALU.mult).then_inc(s["gate_b"], 1)
            dve.wait_ge(s["gate_b"], 1)
            nc.vector.tensor_scalar(gate_s[:], gate_s[:], -1.0, None, ALU.add).then_inc(s["gate_b"], 1)
            dve.wait_ge(s["gate_b"], 2)
            nc.vector.tensor_tensor(gate_m[:], gate, gate_s[:], ALU.mult).then_inc(s["gate_c"], 1)
            dve.wait_ge(s["gate_c"], 1)
            nc.vector.scalar_tensor_tensor(gate, gate_m[:], 0.25, gate_s[:], ALU.max, ALU.mult).then_inc(s["gate_ok"], 1)
            dve.wait_ge(s["decay_raw"], 1)
            nc.vector.tensor_scalar(decay[:], decay[:], float(HD) ** -0.5, None, ALU.mult).then_inc(s["decay_ok"], 1)
            qk_lo_of(0, 0)
            qk_lo_of(0, 1, ps_a)
            dve.wait_ge(s["bo_mm"], 1)
            nc.vector.tensor_tensor(bo2[:], ps_s[1][:, 0:1], vec_sb[:, B_O:B_O + 1], ALU.add).then_inc(s["bo_ok"], 1)
            dve.wait_ge(s["bo_ok"], 1)
            dve.wait_ge(s["gate_ok"], 1)
            nc.vector.tensor_scalar(ga_bo[:], mod_t[:, GA, :], bo2[:, 0:1], None, ALU.mult).then_inc(s["gabo_ok"], 1)
            dve.wait_ge(s["lg_init"], 1)
            dve.wait_ge(s["decay_ok"], 1)
            chunk(0, False, True)
            with dve.Fori(1, NCHUNK - 1) as i:
                chunk(i, True, True)
            chunk(NCHUNK - 1, True, False)

            def y_add(c):
                dve.wait_ge(s["yx_done"], c + 1)
                xs = x_all[:, bass.ds(c * TT, TT), :]
                nc.vector.tensor_tensor(xs, xs, ps_x[:].rearrange("p (t d) -> p t d", t=TT),
                                        ALU.add).then_inc(s["y_added"], 1)

            def ffn(i, tail):
                for u in range(NU):
                    r = u % FR
                    shared = u == NU - 1
                    dve.wait_ge(s["silu_done"], i * NU + u + 1)
                    dve.wait_ge(s["up_done"], i * NU + u + 1)
                    if not (tail and u < FR):
                        dve.wait_ge(s["alo_ok"], i * NU + u + 1 - FR)
                    dst = act if shared else act_u
                    nc.vector.tensor_tensor(dst[:, r, :], act_g[:, r, :], ps_gu[(2 * u + 1) % FR][:],
                                            ALU.mult).then_inc(s["act_ok" if shared else "mul_done"], 1)
                    if not shared:
                        dve.wait_ge(s["mul_done"], i * ROUTED + u + 1)
                        dve.wait_ge(s["cb_done"], i * ROUTED + u + 1)
                        nc.vector.tensor_tensor(act[:, r, :], act_u[:, r, :], ps_c[:], ALU.mult).then_inc(s["act_ok"], 1)
                    if u == 3 and not tail:
                        y_add(i - 1)
                    if tail:
                        c = NCHUNK - 1
                        if u == 0:
                            norm(c, 2, False)
                        if u == 1:
                            norm(c, 3, False)
                        if u == 4:
                            residual(c)
                            ln_stats(c, stats2, "stats2_ok")
                            ln_mean(c, stats2, mv2, "stats2_ok", "mv2_ok")
                        if u == 5:
                            ln_apply(c, mv2, rstd2, xn2, "rstd2_ok", "xn2_ok")
                        if u == 6:
                            h2_lo_of(c)
                        if u == 7:
                            for stage in (r_take, r_top, r_shift, r_fill, r_strike):
                                stage(c)
                        if u == 8:
                            for stage in (r_sum, r_mask, r_inverse, r_keep, r_weight, r_part0, r_rest,
                                          r_part1, r_part2):
                                stage(c)

            ffn(0, True)
            with dve.Fori(1, NCHUNK) as i:
                ffn(i, False)
            y_add(NCHUNK - 1)

        @block.tensor
        def _(pe):
            def mm(o, l, r, start=True, stop=True, check=True, transpose=False):
                return nc.tensor.matmul(o, l, r, start=start, stop=stop, skip_group_check=not check,
                                        is_transpose=transpose or None)

            def transpose4(dst, src):
                for t in range(TT):
                    last = mm(dst[:, t * P:t * P + P], src[:, t, :], id_f[:], transpose=True)
                return last

            def tiles(ap):
                return ap[:].rearrange("p (t k) -> p t k", t=TT)

            def lnt(c):
                pe.wait_ge(s["xn_ok"], c + 1)
                transpose4(ps_b, xn).then_inc(s["lnt_done"], 1)

            def project(c, i, ps=ps_b):
                pe.wait_ge(s["h_ok"], c + 1)
                mm(ps[:], wa_sb[:, (W_Q, W_K)[i], :], h_t[:]).then_inc(s["qk_mm"], 1)

            def project_v(c):
                pe.wait_ge(s["qk_lo_ok"], c * 2 + 2)
                for t in range(TT):
                    last = mm(ps_b[:, t * P:t * P + P], h_t[:, t * P:t * P + P], wa_sb[:, W_V, :])
                last.then_inc(s["v_mm"], 1)

            def scores(i, n, prev):
                g, b, j = n // 8, n // QUAD % BPC, n % QUAD
                if n % 8 == 0:
                    pe.wait_ge(s_st[g], (i + 1) * STACK)
                if prev or n >= SB:
                    pe.wait_ge(s["ttr_done"], i * STEPS + score_bank_before(n) + 1)
                rows = slice(32 * j, 32 * j + 32)
                for t in range(BPC):
                    q0 = b * SEQ + t * P
                    last = mm(ps_s[score_bank(n)][:, t * SEQ:t * SEQ + SEQ], qk_st[rows, 0, g, q0:q0 + P],
                              qk_st[rows, 1, g, b * SEQ:b * SEQ + SEQ])
                last.then_inc(s["s_done"], 1)

            def turn(i, n, later):
                pe.wait_ge(s["nd_done"], i * STEPS + n + 1)
                if later or n >= 2:
                    pe.wait_ge(s["exp_done"], i * STEPS + n - 1)
                for kt in range(BPC):
                    for qt in range(BPC):
                        at = kt * SEQ + qt * P
                        last = mm(ps_t[n % 2][:, at:at + P], sc[:, n % RING, qt, kt * P:kt * P + P], id_f[:],
                                  transpose=True)
                last.then_inc(s["t_done"], 1)

            def values(i, q, later):
                g, b = q // BPC, q % BPC
                pe.wait_ge(s["exp_done"], i * STEPS + QUAD * q + QUAD)
                if b == 0:
                    pe.wait_ge(s["vgrp_ok"], i * NG + g + 1)
                    if later or g >= 1:
                        pe.wait_ge(s["ot_ok"], i * NG + g)
                for kt in range(BPC):
                    for j in range(QUAD):
                        last = mm(ps_o[VW * j:VW * j + VW, b * SEQ:b * SEQ + SEQ],
                                  v_one[:, b * BPC + kt, g, j, :], pr[:, (QUAD * q + j) % RING, kt, :],
                                  start=kt == 0, stop=kt == BPC - 1, check=False)
                last.then_inc(s["pv_done"], 1)

            def by_token(c, g):
                pe.wait_ge(s["ot_ok"], c * NG + g + 1)
                transpose4(ps_a, o_t[:, g % 2, :].rearrange("p (t k) -> p t k", t=TT)).then_inc(s["c_done"], 1)

            def attn_turn(c):
                pe.wait_ge(s["norm_ok"], (c + 1) * NG)
                transpose4(ps_b, attn[:].rearrange("p t g j d -> p t (g j d)")).then_inc(s["at_done"], 1)

            def project_o(c):
                pe.wait_ge(s["at_ok"], c + 1)
                mm(ps_a[:], wa_sb[:, W_O, :], attn_t[:]).then_inc(s["wo_done"], 1)

            def res_turn(c):
                pe.wait_ge(s["rt_ok"], c + 1)
                transpose4(ps_a, tiles(res_t)).then_inc(s["rx_done"], 1)

            def ln2t(c):
                pe.wait_ge(s["xn2_ok"], c + 1)
                transpose4(ps_a, xn2).then_inc(s["ln2t_done"], 1)

            def router(c):
                pe.wait_ge(s["h2t_ok"], c + 1)
                pe.wait_ge(s["h2hi_ok"], c + 1)
                for t in range(TT):
                    last = mm(ps_a[:, t * E:t * E + E], h2_t[:, t * P:t * P + P], wr_sb[:])
                last.then_inc(s["r_done"], 1)

            def weights_turn(c):
                pe.wait_ge(s["cp_ok"], c + 1)
                begin(pe, c)
                for t in range(TT):
                    last = mm(ps_b[0:3 * E, t * P // 2:t * P // 2 + P // 2].bitcast(BF16),
                              cwp[:, t, :, :].rearrange("p a e -> p (a e)"), id_b[:], transpose=True)
                last.then_inc(s["cwt_done"], 1)

            def chunk(i, prev, nxt):
                for n in range(STEPS):
                    scores(i, n, prev)
                    if n >= LAG_T:
                        turn(i, n - LAG_T, prev)
                    elif prev:
                        turn(i - 1, n - LAG_T + STEPS, True)
                    if n % QUAD == LAG_PV % QUAD:
                        if n >= LAG_PV:
                            values(i, (n - LAG_PV) // QUAD, prev)
                        elif prev:
                            values(i - 1, (n - LAG_PV + STEPS) // QUAD, True)
                    if n == 1 and not prev:
                        project_v(i)
                    if n == 7 and prev:
                        pe.wait_ge(s["norm_ok"], i * NG - 1)
                        by_token(i - 1, 3)
                    if n == 9 and prev:
                        pe.wait_ge(s["v_ok"], i + 1)
                        attn_turn(i - 1)
                    if n == 11 and prev:
                        project_o(i - 1)
                    if n == 12 and nxt:
                        if prev:
                            pe.wait_ge(s["at_ok"], i)
                        else:
                            pe.wait_ge(s["v_ok"], 1)
                        lnt(i + 1)
                    if n == 13 and prev:
                        res_turn(i - 1)
                    if n == 14 and nxt:
                        project(i + 1, 0)
                    if n == 15:
                        if prev:
                            pe.wait_ge(s["x2_ok"], i)
                        by_token(i, 0)
                    if n == 17 and nxt:
                        pe.wait_ge(s["qk_lo_ok"], i * 2 + 3)
                        project(i + 1, 1)
                    if n == 18 and prev:
                        pe.wait_ge(s["norm_ok"], i * NG + 1)
                        ln2t(i - 1)
                    if n == 20 and nxt:
                        project_v(i + 1)
                    if n == 21 and prev:
                        router(i - 1)
                    if n == 23:
                        if prev:
                            pe.wait_ge(s["lg_ok"], i)
                        else:
                            pe.wait_ge(s["norm_ok"], 1)
                        by_token(i, 1)
                    if n == 30 and prev:
                        if nxt:
                            pe.wait_ge(s["v_ok"], i + 2)
                        weights_turn(i - 1)
                    if n == 31:
                        pe.wait_ge(s["norm_ok"], i * NG + 2)
                        by_token(i, 2)

            pe.wait_ge(s["ld_mod"], 32)
            pe.wait_ge(s["silu_ok"], 1)
            for k, m in enumerate((0, 3, 1, 4, 2, 5)):
                last = mm(ps_s[0][:, k * NB:k * NB + NB], wmod_sb[:, m, :], silu_c[:])
            last.then_inc(s["modt_mm"], 1)
            pe.wait_ge(s["ld_attn"], 48)
            mm(ps_s[1][:, 0:1], wa_sb[:, W_O, :], vec_sb[:, B_V:B_V + 1]).then_inc(s["bo_mm"], 1)
            lnt(0)
            project(0, 0)
            project(0, 1, ps_a)
            pe.wait_ge(s["gabo_ok"], 1)
            pe.wait_ge(s["idb_ok"], 1)
            chunk(0, False, True)
            with pe.Fori(1, NCHUNK - 1) as i:
                chunk(i, True, True)
            chunk(NCHUNK - 1, True, False)
            for n in range(STEPS - LAG_T, STEPS):
                turn(NCHUNK - 1, n, True)
                if n == STEPS - LAG_T + 1:
                    values(NCHUNK - 1, QUADS - 2, True)

            pe.wait_ge(s["wlo_ok"], NU)
            pe.wait_ge(s["sele_ok"], 1)

            def part(i, u, half, done):
                dst, hi, lo = ps_gu[(2 * u + half) % FR], of_chunk(h2_hi, i), of_chunk(h2_lo, i)
                mm(dst[:], wgu_hi[:, u, half, :], hi, stop=False)
                mm(dst[:], wgu_lo[:, u, half, :], hi, start=False, stop=False)
                mm(dst[:], wgu_hi[:, u, half, :], lo, start=False).then_inc(s[done], 1)

            def down(i, u, first):
                pe.wait_ge(s["alo_ok"], i * NU + u + 1)
                if u == 0 and not first:
                    pe.wait_ge(s["yt_ok"], i)
                hi, lo = act_hi[:, u % FR, :], act_lo[:, u % FR, :]
                mm(ps_y[:], wd_hi[:, u, :], hi, start=u == 0, stop=False, check=False)
                mm(ps_y[:], wd_lo[:, u, :], hi, start=False, stop=False, check=False)
                mm(ps_y[:], wd_hi[:, u, :], lo, start=False, stop=u == NU - 1, check=False).then_inc(s["down_done"], 1)

            def y_turn(c):
                pe.wait_ge(s["yt_ok"], c + 1)
                transpose4(ps_x, tiles(y_t)).then_inc(s["yx_done"], 1)

            def ffn(i, tail):
                for u in range(NU):
                    if not (tail and u < 2):
                        if u == 1:
                            pe.wait_ge(s["act_ok"], i * NU)
                        else:
                            pe.wait_ge(s["mul_done"], i * ROUTED + (u - 1 if u else 0))
                    part(i, u, 0, "gate_done")
                    if not (tail and u == 0):
                        pe.wait_ge(s["silu_done"], i * NU + u)
                    part(i, u, 1, "up_done")
                    if tail and u == 0:
                        values(NCHUNK - 1, QUADS - 1, True)
                    if u < ROUTED:
                        if tail and u == 0:
                            pe.wait_ge(s["exp_done"], NCHUNK * STEPS)
                        else:
                            pe.wait_ge(s["act_ok"], i * NU + u)
                        begin(pe, i)
                        mm(ps_c[:], sele_b[:, u, :], of_chunk(cw_t, i)).then_inc(s["cb_done"], 1)
                    if u >= LAG_D:
                        down(i, u - LAG_D, tail)
                    elif not tail:
                        down(i - 1, u - LAG_D + NU, False)
                    if u == 2 and not tail:
                        y_turn(i - 1)
                    if tail:
                        c = NCHUNK - 1
                        if u == 1:
                            pe.wait_ge(s["norm_ok"], c * NG + 3)
                            by_token(c, 3)
                        if u == 2:
                            pe.wait_ge(s["cwt_ok"], c)
                            attn_turn(c)
                        if u == 3:
                            project_o(c)
                        if u == 4:
                            res_turn(c)
                        if u == 6:
                            ln2t(c)
                        if u == 7:
                            router(c)
                if tail:
                    weights_turn(NCHUNK - 1)

            ffn(0, True)
            pe.wait_ge(s["cwt_ok"], NCHUNK)
            pe.wait_ge(s["h2lo_ok"], NCHUNK)
            with pe.Fori(1, NCHUNK) as i:
                ffn(i, False)
            for u in range(NU - LAG_D, NU):
                down(NCHUNK - 1, u, False)
            y_turn(NCHUNK - 1)


_OUT = ("out_0_dram", (NB * SEQ, D))


def kernel(**inputs):
    import concourse.bacc as bacc
    from concourse.bass_utils import run_bass_kernel_spmd

    a = {k.replace("L0_attn_", "").replace("L0_ffn_", "").replace("L0_", ""): np.asarray(v)
         for k, v in inputs.items()}

    def by_unit(w, shared):
        w = w.reshape(E // 2, 2, D, FE).transpose(2, 0, 1, 3).reshape(D, E // 2, P)
        return np.concatenate([w, shared.reshape(D, 1, P)], axis=1)

    w_gu = np.stack([by_unit(a["Wg"], a["Sg"]), by_unit(a["Wu"], a["Su"])], axis=2)
    w_d = np.concatenate([a["Wd"].reshape(E // 2, P, D), a["Sd"].reshape(1, P, D)]).transpose(1, 0, 2)

    w_attn = np.stack([a["Wq"].T, a["Wk"].T, a["Wv"].T, a["Wo"].T], axis=1)
    vecs = np.stack([a["bq"], a["bk"], a["bv"], a["bo"]], axis=1)

    tok = np.arange(SEQ)
    lag = np.abs(tok[:, None] - tok[None, :]).astype(np.float32).reshape(BPC, P, SEQ).transpose(1, 0, 2)
    ident = np.eye(P, dtype=np.float32)
    sel_e = np.zeros((3, E, ROUTED, P), np.float32)
    for e in range(E):
        sel_e[:, e, e // 2, (e % 2) * FE:(e % 2) * FE + FE] = 1.0

    arrays = {
        "x": a["x"].reshape(NB * SEQ, D), "c_t": a["c"].T, "w_attn": w_attn, "vecs": vecs,
        "alpha": a["alpha"].reshape(1, 1), "w_r": a["Wr"], "w_gu": w_gu, "w_d": w_d,
        "w_mod": a["wmod"].reshape(D, 6, D), "lag": lag, "ident": ident,
        "sel_e": sel_e.reshape(3 * E, ROUTED, P),
    }
    arrays = {f"in_{k}": np.ascontiguousarray(v) for k, v in arrays.items()}
    nc = bacc.Bacc("TRN2", target_bir_lowering=False, num_devices=1)
    args = [nc.dram_tensor(k, v.shape, mybir.dt.from_np(v.dtype), kind="ExternalInput").ap()
            for k, v in arrays.items()]
    args.append(nc.dram_tensor(_OUT[0], _OUT[1], F32, kind="ExternalOutput").ap())
    build(nc, *args)
    r = run_bass_kernel_spmd(nc, [arrays], core_ids=[0])
    return r.results[0][_OUT[0]].reshape(NB, SEQ, D)
```
